# Optimizing a Trainium2 kernel written in Bass

```python
import numpy as np
import jax
import jax.numpy as jnp

def _softmax(x, axis=-1):
    return jax.nn.softmax(x, axis=axis)

def _gelu(x):
    return jax.nn.gelu(x, approximate=True)

def _silu(x):
    return jax.nn.silu(x)

def _sigmoid(x):
    return jax.nn.sigmoid(x)

def _layernorm(x, axis=-1, eps=1e-05):
    m = jnp.mean(x, axis=axis, keepdims=True)
    v = jnp.var(x, axis=axis, keepdims=True)
    return (x - m) / jnp.sqrt(v + eps)

def _scatter_add(tgt, idx, src, axis=0):
    return tgt.at[idx].add(src)

def _segment_sum(src, seg, n):
    return jax.ops.segment_sum(src, seg, n)
kernel_name = 'mk_vit_tower_d2_tok_img1024_r4_ea8d11'

def setup_inputs(seed: int=0):
    np.random.seed(seed)
    _w = jnp.asarray

    def _rec_inputs():
        import jax
        import jax.numpy as jnp
        _rk = jax.random.key(seed)
        x = -0.00011082 + 0.999858 * jax.random.normal(jax.random.fold_in(_rk, 1), (8, 5, 128, 128), jnp.float32)
        return x
    x = _rec_inputs()

    def _L0_tok_setup():
        import jax, jax.numpy as jnp
        import numpy as np
        PATCH = 8
        EPS = 1e-05

        def _patchify(x):
            B, C, H, Wd = x.shape
            p = PATCH
            x = x.reshape(B, C, H // p, p, Wd // p, p)
            x = x.transpose(0, 2, 4, 1, 3, 5)
            return x.reshape(B, H // p * (Wd // p), C * p * p)
        key = jax.random.key(seed)
        k1, k2 = jax.random.split(key)
        B, C, H, W_ = (32, 5, 128, 128)
        in_feat, embed_dim = (C * PATCH * PATCH, 256)
        x = jax.random.normal(k1, (B, C, H, W_), dtype=jnp.float32)
        W = jax.random.normal(k2, (in_feat, embed_dim), dtype=jnp.float32) * (1.0 / np.sqrt(in_feat))
        gamma = jnp.ones((embed_dim,), dtype=jnp.float32)
        return {'x': x, 'W': W, 'gamma': gamma}
    _L0_tok_all = _L0_tok_setup()
    _L0_tok_in = {k: v for k, v in _L0_tok_all.items() if k in ('W', 'gamma')}
    del _L0_tok_all

    def _L0_attn_setup():
        import jax, jax.numpy as jnp
        import numpy as np
        S, B, D, H, C = (256, 1, 256, 16, 64)
        DH = D // H

        def _xavier(key, shape):
            fan_in, fan_out = (shape[1], shape[0])
            a = float(np.sqrt(6.0 / (fan_in + fan_out)))
            return jax.random.uniform(key, shape, jnp.float32, -a, a)
        key = jax.random.key(seed)
        ks = jax.random.split(key, 7)
        x = jax.random.normal(ks[0], (S, B, D), jnp.float32)
        q_c = _xavier(ks[1], (C, D))
        beta = jnp.zeros((H,), jnp.float32)
        Wq = _xavier(ks[2], (D, D))
        bq = jnp.zeros((D,), jnp.float32)
        Wk = _xavier(ks[3], (D, D))
        bk = jnp.zeros((D,), jnp.float32)
        Wv = _xavier(ks[4], (D, D))
        bv = jnp.zeros((D,), jnp.float32)
        Wo = _xavier(ks[5], (D, D))
        bo = jnp.zeros((D,), jnp.float32)
        return {'x': x, 'q_c': q_c, 'beta': beta, 'Wq': Wq, 'bq': bq, 'Wk': Wk, 'bk': bk, 'Wv': Wv, 'bv': bv, 'Wo': Wo, 'bo': bo}
    _L0_attn_all = _L0_attn_setup()
    _L0_attn_in = {k: v for k, v in _L0_attn_all.items() if k in ('q_c', 'beta', 'Wq', 'bq', 'Wk', 'bk', 'Wv', 'bv', 'Wo', 'bo')}
    del _L0_attn_all

    def _L0_ffn_setup():
        import jax, jax.numpy as jnp
        import numpy as np
        B, T, C = (4, 512, 256)
        E = 8
        K = 2
        H = 352
        HS = 352 * 2
        key = jax.random.key(seed)
        k = jax.random.split(key, 8)
        s = 0.02
        return {'x': jax.random.normal(k[0], (B, T, C), jnp.float32), 'Wg': jax.random.normal(k[1], (C, E), jnp.float32) * s, 'W1': jax.random.normal(k[2], (E, C, H), jnp.float32) * s, 'W2': jax.random.normal(k[3], (E, C, H), jnp.float32) * s, 'W3': jax.random.normal(k[4], (E, H, C), jnp.float32) * s, 'Ws1': jax.random.normal(k[5], (C, HS), jnp.float32) * s, 'Ws2': jax.random.normal(k[6], (C, HS), jnp.float32) * s, 'Ws3': jax.random.normal(k[7], (HS, C), jnp.float32) * s}
    _L0_ffn_all = _L0_ffn_setup()
    _L0_ffn_in = {k: v for k, v in _L0_ffn_all.items() if k in ('Wg', 'W1', 'W2', 'W3', 'Ws1', 'Ws2', 'Ws3')}
    del _L0_ffn_all

    def _L1_attn_setup():
        import jax, jax.numpy as jnp
        import numpy as np
        EPS = 1e-08
        key = jax.random.key(seed)
        x = jax.random.normal(key, (64, 200, 256), dtype=jnp.float32)
        return {'x': x}
    _L1_attn_all = _L1_attn_setup()
    _L1_attn_in = {k: v for k, v in _L1_attn_all.items() if k in ()}
    del _L1_attn_all

    def _L1_ffn_setup():
        import jax, jax.numpy as jnp
        import numpy as np
        D_MODEL = 256
        key = jax.random.key(seed)
        k_x, k_w, k_a1, k_a2 = jax.random.split(key, 4)
        x = jax.random.normal(k_x, (4, 512, D_MODEL), dtype=jnp.float32)
        weight = jax.random.normal(k_w, (D_MODEL, D_MODEL), dtype=jnp.float32) * 0.02
        aux_weight1 = jax.random.normal(k_a1, (D_MODEL, D_MODEL), dtype=jnp.float32) * 0.02
        aux_weight2 = jax.random.normal(k_a2, (D_MODEL, D_MODEL), dtype=jnp.float32) * 0.02
        bias = jnp.zeros((D_MODEL,), dtype=jnp.float32)
        return {'x': x, 'weight': weight, 'aux_weight1': aux_weight1, 'aux_weight2': aux_weight2, 'bias': bias}
    _L1_ffn_all = _L1_ffn_setup()
    _L1_ffn_in = {k: v for k, v in _L1_ffn_all.items() if k in ('weight', 'aux_weight1', 'aux_weight2', 'bias')}
    del _L1_ffn_all
    return {'x': x, 'L0_tok_W': _L0_tok_in['W'], 'L0_tok_gamma': _L0_tok_in['gamma'], 'L0_attn_q_c': _L0_attn_in['q_c'], 'L0_attn_beta': _L0_attn_in['beta'], 'L0_attn_Wq': _L0_attn_in['Wq'], 'L0_attn_bq': _L0_attn_in['bq'], 'L0_attn_Wk': _L0_attn_in['Wk'], 'L0_attn_bk': _L0_attn_in['bk'], 'L0_attn_Wv': _L0_attn_in['Wv'], 'L0_attn_bv': _L0_attn_in['bv'], 'L0_attn_Wo': _L0_attn_in['Wo'], 'L0_attn_bo': _L0_attn_in['bo'], 'L0_ffn_Wg': _L0_ffn_in['Wg'], 'L0_ffn_W1': _L0_ffn_in['W1'], 'L0_ffn_W2': _L0_ffn_in['W2'], 'L0_ffn_W3': _L0_ffn_in['W3'], 'L0_ffn_Ws1': _L0_ffn_in['Ws1'], 'L0_ffn_Ws2': _L0_ffn_in['Ws2'], 'L0_ffn_Ws3': _L0_ffn_in['Ws3'], 'L1_ffn_weight': _L1_ffn_in['weight'], 'L1_ffn_aux_weight1': _L1_ffn_in['aux_weight1'], 'L1_ffn_aux_weight2': _L1_ffn_in['aux_weight2'], 'L1_ffn_bias': _L1_ffn_in['bias']}

def reference(x, L0_tok_W, L0_tok_gamma, L0_attn_q_c, L0_attn_beta, L0_attn_Wq, L0_attn_bq, L0_attn_Wk, L0_attn_bk, L0_attn_Wv, L0_attn_bv, L0_attn_Wo, L0_attn_bo, L0_ffn_Wg, L0_ffn_W1, L0_ffn_W2, L0_ffn_W3, L0_ffn_Ws1, L0_ffn_Ws2, L0_ffn_Ws3, L1_ffn_weight, L1_ffn_aux_weight1, L1_ffn_aux_weight2, L1_ffn_bias):
    import jax
    import jax.numpy as jnp

    def _L0_tok_ref(x, W, gamma):
        import jax, jax.numpy as jnp
        import numpy as np
        PATCH = 8
        EPS = 1e-05

        def _patchify(x):
            B, C, H, Wd = x.shape
            p = PATCH
            x = x.reshape(B, C, H // p, p, Wd // p, p)
            x = x.transpose(0, 2, 4, 1, 3, 5)
            return x.reshape(B, H // p * (Wd // p), C * p * p)
        tokens = _patchify(x)
        h = jnp.einsum('bnf,fd->bnd', tokens, W)
        mu = jnp.mean(h, axis=-1, keepdims=True)
        var = jnp.mean(jnp.square(h - mu), axis=-1, keepdims=True)
        out = (h - mu) * jax.lax.rsqrt(var + EPS) * gamma
        return out

    def _L0_attn_ref(x, q_c, beta, Wq, bq, Wk, bk, Wv, bv, Wo, bo):
        import jax, jax.numpy as jnp
        import numpy as np
        S, B, D, H, C = (256, 1, 256, 16, 64)
        DH = D // H

        def _xavier(key, shape):
            fan_in, fan_out = (shape[1], shape[0])
            a = float(np.sqrt(6.0 / (fan_in + fan_out)))
            return jax.random.uniform(key, shape, jnp.float32, -a, a)
        s_len, bsz, d_model = x.shape
        h, dh = (H, DH)
        c_len = q_c.shape[0]

        def proj(W, b):
            return (x @ W.T + b).reshape(s_len, bsz, h, dh).transpose(1, 2, 0, 3)
        q = proj(Wq, bq)
        k = proj(Wk, bk)
        v = proj(Wv, bv)
        qc = q_c.reshape(c_len, h, dh).transpose(1, 0, 2)
        cw = jnp.einsum('hcd,bhsd->bhcs', qc, k)
        cw = jnp.exp(cw - jnp.max(cw, axis=-1, keepdims=True))
        norm = jnp.cumsum(cw, axis=-1)
        kv = jnp.concatenate([k, v], axis=-1)
        kv_c = jnp.cumsum(cw[..., None] * kv[:, :, None, :, :], axis=3) / norm[..., None]
        k_c, v_c = (kv_c[..., :dh], kv_c[..., dh:])
        q = q / (jnp.sqrt(jnp.float32(dh)) * jnp.exp(beta)[None, :, None, None])
        sw = jax.nn.softmax(jnp.einsum('bhsd,bhcsd->bhsc', q, k_c), axis=-1)
        o = jnp.einsum('bhsc,bhcsd->bhsd', sw, v_c)
        o = o.transpose(2, 0, 1, 3).reshape(s_len, bsz, d_model)
        return o @ Wo.T + bo

    def _L0_ffn_ref(x, Wg, W1, W2, W3, Ws1, Ws2, Ws3):
        import jax, jax.numpy as jnp
        import numpy as np
        B, T, C = (4, 512, 256)
        E = 8
        K = 2
        H = 352
        HS = 352 * 2
        b, t, c = x.shape
        xf = x.reshape(-1, c)
        n = xf.shape[0]
        router = xf @ Wg
        top_logits, idx = jax.lax.top_k(router, K)
        probs = jax.nn.softmax(top_logits.astype(jnp.float32), axis=-1).astype(x.dtype)
        w = jnp.zeros((n, E), x.dtype).at[jnp.arange(n)[:, None], idx].add(probs)
        h = jax.nn.silu(jnp.einsum('tc,ech->eth', xf, W1)) * jnp.einsum('tc,ech->eth', xf, W2)
        y = jnp.einsum('eth,ehc,te->tc', h, W3, w)
        y = y.reshape(b, t, c)
        hs = jax.nn.silu(xf @ Ws1) * (xf @ Ws2)
        y = y + (hs @ Ws3).reshape(b, t, c)
        return y

    def _L1_attn_ref(x):
        import jax, jax.numpy as jnp
        import numpy as np
        EPS = 1e-08
        norms = jnp.linalg.norm(x, axis=-1)
        dots = jnp.einsum('bil,bjl->bij', x, x)
        sim = dots / jnp.maximum(norms[:, :, None] * norms[:, None, :], EPS)
        atten = jax.nn.softmax(sim, axis=-1)
        out = jnp.einsum('bij,bjl->bil', atten, x) + x
        return out

    def _L1_ffn_ref(x, weight, aux_weight1, aux_weight2, bias):
        import jax, jax.numpy as jnp
        import numpy as np
        D_MODEL = 256
        h = jnp.einsum('btc,cd->btd', x, weight)
        h = jnp.einsum('btc,cd->btd', h, aux_weight1)
        h = jnp.einsum('btc,cd->btd', h, aux_weight2)
        return jnp.tanh(h + bias)
    h = _L0_tok_ref(x, L0_tok_W, L0_tok_gamma)
    h = h + _L0_attn_ref(_layernorm(h, axis=-1), L0_attn_q_c, L0_attn_beta, L0_attn_Wq, L0_attn_bq, L0_attn_Wk, L0_attn_bk, L0_attn_Wv, L0_attn_bv, L0_attn_Wo, L0_attn_bo)
    h = h + _L0_ffn_ref(_layernorm(h, axis=-1), L0_ffn_Wg, L0_ffn_W1, L0_ffn_W2, L0_ffn_W3, L0_ffn_Ws1, L0_ffn_Ws2, L0_ffn_Ws3)
    h = h + _L1_attn_ref(_layernorm(h, axis=-1))
    h = h + _L1_ffn_ref(_layernorm(h, axis=-1), L1_ffn_weight, L1_ffn_aux_weight1, L1_ffn_aux_weight2, L1_ffn_bias)
    return h

_drawn_inputs = setup_inputs


def setup_inputs(seed=0):
    import zlib

    import numpy as np

    out = dict(_drawn_inputs(seed))
    spreads = {'L0_tok_gamma': (1.0, 0.2),
     'L0_attn_beta': (0.0, 0.8),
     'L0_attn_bq': (0.0, 0.8),
     'L0_attn_bk': (0.0, 2.0),
     'L0_attn_bv': (0.0, 0.1),
     'L0_attn_bo': (0.0, 0.1),
     'L1_ffn_bias': (0.0, 0.621)}
    factors = {'L0_attn_q_c': 4.3,
     'L0_attn_Wq': 4.702,
     'L0_attn_Wk': 3.095,
     'L0_ffn_Wg': 5.585,
     'L0_ffn_W1': 4.858,
     'L0_ffn_W2': 4.816,
     'L0_ffn_W3': 4.817,
     'L1_ffn_weight': 3.91,
     'L1_ffn_aux_weight1': 3.935,
     'L1_ffn_aux_weight2': 3.925,
     'L0_ffn_Ws1': 5.176,
     'L0_ffn_Ws2': 5.12,
     'L0_ffn_Ws3': 5.144}
    for name, (base, spread) in spreads.items():
        noise = np.random.default_rng([zlib.crc32(name.encode()), seed]).standard_normal(out[name].shape)
        drawn = base * np.exp(spread * noise) if base else spread * noise
        out[name] = jnp.asarray(drawn.astype(out[name].dtype))
    for name, factor in factors.items():
        out[name] = (out[name] * factor).astype(out[name].dtype)
    return out
```

```python
import numpy as np
import concourse.bass as bass
from concourse import mybir
from contextlib import ExitStack

F32 = mybir.dt.float32
I32 = mybir.dt.int32
U32 = mybir.dt.uint32
ALU = mybir.AluOpType
ACT = mybir.ActivationFunctionType
AX = mybir.AxisListType

P = 128
S = 8
N = 256
T = S * N
NT = T // P
D = 256
KD = D // P
FEAT = 320
KF = 3
FK = [P, P, FEAT - 2 * P]
H = 16
DH = D // H
C = 64
HP = H // 2
VW = DH + 1
E = 8
HE = 352
KH = 3
HK = [P, P, HE - 2 * P]
TOP = 2
NS = (TOP * T + E * (P - 1)) // P
RC = NT + E + NS
ONEHOT, DIFF = 13, 14
EPS = 1e-5


def ge(eng, sem, value):
    if isinstance(value, int) and value <= 0:
        return
    eng.wait_ge(sem, value)


def bc(ap, shape):
    return ap.unsqueeze(2).broadcast_to(shape)


def steps(eng, body, first, last):
    for k in range(first, 2):
        body(k, k % 2)
    with eng.Fori(1, NT // 2 - 1) as i:
        body(i * 2, 0)
        body(i * 2 + 1, 1)
    for k in range(NT - 2, last):
        body(k, k % 2)


def has(k, lo, hi):
    return not isinstance(k, int) or lo <= k < hi


def attention_stage(nc, ctx, io, keep):

    def sb(name, shape, dt=F32):
        return ctx.enter_context(nc.sbuf_tensor(name, shape, dt))

    def sem(name):
        return ctx.enter_context(nc.semaphore(name))

    wtok = sb("wtok", [P, KF, D])
    gamma = sb("gamma", [P, D])
    wq = sb("wq", [P, KD, D])
    wk = sb("wk", [P, KD, D])
    wv = sb("wv", [P, KD, D])
    wo = sb("wo", [P, KD, D])
    qc = sb("qc", [P, HP, P])
    small = sb("small", [P, 8])
    bv = sb("bv", [P, D])
    bo = sb("bo", [P, D])
    wg = sb("wg", [P, KD, E])
    ident, mask = keep["ident"], keep["mask"]
    h2_all, x2_all, x2T_all, lg_all = keep["h2"], keep["x2"], keep["x2T"], keep["lg"]

    qscale = sb("qscale", [P, KD, 2])
    expb = sb("expb", [P, KD])
    mhalf, touch = sb("mhalf", [P, 1]), sb("touch", [P, 1])
    xt = sb("xt", [P, 2, KF, P])
    st0, mv0, ve0, r0 = sb("st0", [P, 6]), sb("mv0", [P, 2]), sb("ve0", [P, 1]), sb("r0", [P, 1])
    st1, mv1, ve1, r1 = sb("st1", [P, 6]), sb("mv1", [P, 2]), sb("ve1", [P, 1]), sb("r1", [P, 1])
    st2, mv2, ve2, r2 = sb("st2", [P, 6]), sb("mv2", [P, 2]), sb("ve2", [P, 1]), sb("r2", [P, 1])
    h0 = sb("h0", [P, D])
    h1 = sb("h1", [P, 2, D])
    x1 = sb("x1", [P, D])
    x1T = sb("x1T", [P, KD, P])
    qz = sb("qz", [P, KD, 2, P])
    kT = sb("kT", [P, KD, P])
    v1 = sb("v1", [P, 2, H, VW])
    mx = sb("mx", [P, P])
    cwd = sb("cwd", [P, HP, P])
    cwT = sb("cwT", [P, 2, HP, P])
    cw = sb("cw", [P, HP * P])
    qkm = sb("qkm", [P, 2, HP, P])
    ln = sb("ln", [P, H * C])
    rn = sb("rn", [P, H * C])
    sc = sb("sc", [P, H, C])
    scm = sb("scm", [P, H])
    scd = sb("scd", [P, H, C])
    ex = sb("ex", [P, H * C])
    w = sb("w", [P, HP, P])
    wT = sb("wT", [P, HP, P])
    am = sb("am", [P, 2, HP, P])
    rz = sb("rz", [P, H])
    on = sb("on", [P, H, DH])
    oT = sb("oT", [P, KD, P])
    yb = sb("yb", [P, D])
    h2 = sb("h2", [P, D])
    x2 = sb("x2", [P, D])
    x2T = sb("x2T", [P, KD, P])

    ps = keep["ps"]
    S0, S1 = ps[:, 0:512], ps[:, 512:1024]
    X, Y, Z = ps[:, 1024:2048], ps[:, 2048:3072], ps[:, 3072:4096]
    pTok, pX1T = S0[:, 0:D], S0[:, D:2 * D]
    pV, pX2T, pY, pOT = S0[:, 0:D], S0[:, 0:D], S0[:, 0:D], S0[:, D:2 * D]
    pQK, pO, pLg = S1, S1[:, 0:H * VW], S1[:, 280:280 + E]

    names = """tok_mm x1_tr qk_mm v_mm cwT_mm qka_mm qkb_mm cw_tr norm_mm s_mm w_tr aa_mm ab_mm o_mm o_tr
        y_mm x2_tr lg_mm  x1T_ok kT_ok ln_ok rn_ok e_ok cwT_ok cw_ok wT_ok oT_ok x2T_ok
        st0_ok mv0_ok st1_ok mv1_ok st2_ok mv2_ok ve0_ok r0_ok ve1_ok r1_ok ve2_ok r2_ok h0_ok h1_ok
        x1_ok qz_ok v_ok mx_ok cwd_ok qkma_ok qkmb_ok sc_ok scm_ok scd_ok ama_ok amb_ok rz_ok on_ok
        yb_ok h2_ok x2_ok lg_ok w_ok x2c_ok x2Tc_ok h2c_ok""".split()
    s = {n: sem("A_" + n) for n in names}
    x_in = [sem("A_x_in0"), sem("A_x_in1")]
    w_in = sem("A_w_in")
    c_ok = sem("A_c_ok")
    z_ok = sem("A_z_ok")

    loads = [(wtok, io["wtok"]), (gamma, io["gamma"].partition_broadcast(P)), (wq, io["wq"]), (wk, io["wk"]),
             (wv, io["wv"]), (small, io["small"]), (bv, io["bv"].partition_broadcast(P)), (ident, io["ident"]),
             (mask, io["mask"]), (qc, io["qc"]), (wo, io["wo"]), (bo, io["bo"].partition_broadcast(P)),
             (wg, io["wg"])]
    ALL_IN = 16 * len(loads)

    with nc.Block() as block:

        @block.sync
        def _(sp):
            sp.dma_start(xt[:, 0], io["x"][0]).then_inc(x_in[0], 16)
            for dst, src in loads[:2]:
                sp.dma_start(dst[:], src).then_inc(w_in, 16)
            sp.dma_start(xt[:, 1], io["x"][1]).then_inc(x_in[1], 16)
            for dst, src in loads[2:]:
                sp.dma_start(dst[:], src).then_inc(w_in, 16)

            def load(t, par):
                ge(sp, s["tok_mm"], t - 1)
                sp.dma_start(xt[:, par], io["x"][t]).then_inc(x_in[par], 16)

            sp.dma_start(keep["ws12"][:], io["ws12"]).then_inc(keep["ws_in"], 16)
            sp.dma_start(keep["ws3"][:], io["ws3"]).then_inc(keep["ws_in"], 16)
            sp.wait_ge(z_ok, 1)
            sp.dma_start(keep["xs"].rearrange("(p j) d -> p j d", p=P),
                         keep["zeros"][:, :].unsqueeze(1).broadcast_to([P, NS, D])).then_inc(keep["xs_zero"], 16)
            with sp.Fori(1, NT // 2) as i:
                load(i * 2, 0)
                load(i * 2 + 1, 1)
            sp.wait_ge(keep["ws_in"], 32)

        @block.tensor
        def _(pe):
            mm, tr = nc.tensor.matmul, nc.tensor.transpose

            def tok(t, par, half):
                ge(pe, x_in[par], (half + 1) * 16)
                ge(pe, s["h2_ok"], t - 1)
                for c in range(KF):
                    last = mm(pTok, xt[0:FK[c], par, c, :], wtok[0:FK[c], c, :], start=c == 0, stop=c == KF - 1)
                last.then_inc(s["tok_mm"], 1)

            def x1_transpose(t):
                ge(pe, s["x1_ok"], t + 1)
                ge(pe, s["x2T_ok"], t - 1)
                for c in range(KD):
                    last = tr(pX1T[:, c * P:(c + 1) * P], x1[:, c * P:(c + 1) * P], ident[:])
                last.then_inc(s["x1_tr"], 1)

            def project(t):
                ge(pe, s["x1T_ok"], t + 1)
                ge(pe, s["on_ok"], t - 1)
                for n, wt in enumerate((wq, wk)):
                    for m in range(KD):
                        for c in range(KD):
                            last = mm(pQK[:, (2 * n + m) * P:(2 * n + m + 1) * P], wt[:, c, m * P:(m + 1) * P],
                                      x1T[:, c, :], start=c == 0, stop=c == KD - 1)
                last.then_inc(s["qk_mm"], 1)
                for c in range(KD):
                    last = mm(pV, x1T[:, c, :], wv[:, c, :], start=c == 0, stop=c == KD - 1)
                last.then_inc(s["v_mm"], 1)

            def qk(t):
                ge(pe, s["qz_ok"], t + 1)
                ge(pe, s["kT_ok"], t + 1)
                ge(pe, s["cw_ok"], t)
                for half, out in enumerate((Z, X)):
                    if half:
                        ge(pe, s["ln_ok"], t)
                    for j in (0, 1, 4, 5):
                        j += 2 * half
                        at = (j % 2) * 512 + (j // 4) * D
                        rows = slice(32 * (j % 4), 32 * (j % 4) + 32)
                        last = mm(out[:, at:at + D].rearrange("p (e n) -> p e n", e=2), kT[rows, j // 4, :],
                                  qz[rows, j // 4, :, :], start=True, stop=True)
                    last.then_inc(s["qkb_mm" if half else "qka_mm"], 1)

            def cw_logits(t):
                ge(pe, s["sc_ok"], t)
                for j in range(HP):
                    last = mm(Y[:, j * P:(j + 1) * P], qc[:, j, :], kT[:, j // 4, :], start=True, stop=True)
                last.then_inc(s["cwT_mm"], 1)

            def cw_transpose(t):
                ge(pe, s["cwT_ok"], t + 1)
                ge(pe, s["wT_ok"], t)
                for j in range(HP):
                    last = tr(Z[:, j * P:(j + 1) * P], cwT[:, par_of(t), j, :], ident[:])
                last.then_inc(s["cw_tr"], 1)

            def norms(t):
                ge(pe, s["cw_ok"], t + 1)
                ge(pe, s["ama_ok"], t)
                for c in range(2):
                    last = mm(X[:, c * 512:(c + 1) * 512], mask[:], cw[:, c * 512:(c + 1) * 512], start=True, stop=True)
                last.then_inc(s["norm_mm"], 1)

            def scores(t):
                ge(pe, s["qkma_ok"], t + 1)
                ge(pe, s["qkmb_ok"], t + 1)
                ge(pe, s["amb_ok"], t)
                for h in range(H):
                    j, e = h // 2, h % 2
                    last = mm(Y[:, h * C:(h + 1) * C], qkm[:, (j % 4) // 2, (j % 2) * 4 + (j // 4) * 2 + e, :],
                              cw[:, h * C:(h + 1) * C], start=True, stop=True)
                last.then_inc(s["s_mm"], 1)

            def w_transpose(t):
                ge(pe, s["w_ok"], t + 1)
                ge(pe, s["qkma_ok"], t + 2 if not isinstance(t, int) else min(t + 2, NT))
                for j in range(HP):
                    last = tr(Z[:, j * P:(j + 1) * P], w[:, j, :], ident[:])
                last.then_inc(s["w_tr"], 1)

            def weights_of_values(t, par):
                ge(pe, s["wT_ok"], t + 1)
                for half, out in enumerate((X, Y)):
                    if half:
                        ge(pe, s["cwd_ok"], t + 2 if not isinstance(t, int) else min(t + 2, NT))
                    else:
                        ge(pe, s["qkmb_ok"], t + 2 if not isinstance(t, int) else min(t + 2, NT))
                        ge(pe, s["ln_ok"], t + 1)
                    for jj in range(4):
                        for e in range(2):
                            at = e * 512 + jj * P
                            rows = slice(64 * e, 64 * e + 64)
                            last = mm(out[:, at:at + P], cwT[rows, par, 4 * half + jj, :],
                                      wT[rows, 4 * half + jj, :], start=True, stop=True)
                    last.then_inc(s["ab_mm" if half else "aa_mm"], 1)

            def values(t, par):
                ge(pe, s["ama_ok"], t + 1)
                ge(pe, s["amb_ok"], t + 1)
                ge(pe, s["v_ok"], t + 1)
                ge(pe, s["lg_ok"], t)
                for h in range(H):
                    j, e = h // 2, h % 2
                    last = mm(pO[:, h * VW:(h + 1) * VW], am[:, j // 4, e * 4 + j % 4, :], v1[:, par, h, :],
                              start=True, stop=True)
                last.then_inc(s["o_mm"], 1)

            def o_transpose(t):
                ge(pe, s["on_ok"], t + 1)
                ge(pe, s["v_ok"], t + 2 if not isinstance(t, int) else min(t + 2, NT))
                for c in range(KD):
                    last = tr(pOT[:, c * P:(c + 1) * P], on[:, :, :].rearrange("p h d -> p (h d)")[:, c * P:(c + 1) * P],
                              ident[:])
                last.then_inc(s["o_tr"], 1)

            def out_project(t):
                ge(pe, s["oT_ok"], t + 1)
                for c in range(KD):
                    last = mm(pY, oT[:, c, :], wo[:, c, :], start=c == 0, stop=c == KD - 1)
                last.then_inc(s["y_mm"], 1)

            def x2_transpose(t):
                ge(pe, s["x2_ok"], t + 1)
                ge(pe, s["h0_ok"], t + 3 if not isinstance(t, int) else min(t + 3, NT))
                for c in range(KD):
                    last = tr(pX2T[:, c * P:(c + 1) * P], x2[:, c * P:(c + 1) * P], ident[:])
                last.then_inc(s["x2_tr"], 1)

            def router(t):
                ge(pe, s["x2T_ok"], t + 1)
                ge(pe, s["kT_ok"], t + 3 if not isinstance(t, int) else min(t + 3, NT))
                ge(pe, s["on_ok"], t + 1)
                for c in range(KD):
                    last = mm(pLg, x2T[:, c, :], wg[:, c, :], start=c == 0, stop=c == KD - 1)
                last.then_inc(s["lg_mm"], 1)

            par_now = [0]

            def par_of(t):
                return par_now[0]

            def step(k, par):
                par_now[0] = 1 - par
                if has(k, -1, NT - 1):
                    tok(k + 1, 1 - par, half_of(k, par))
                if has(k, 0, NT):
                    norms(k)
                    scores(k)
                if has(k - 1, 0, NT):
                    x2_transpose(k - 1)
                if has(k, -1, NT - 1):
                    x1_transpose(k + 1)
                    project(k + 1)
                    qk(k + 1)
                    cw_logits(k + 1)
                if has(k, 0, NT):
                    w_transpose(k)
                    weights_of_values(k, par)
                if has(k, -1, NT - 1):
                    cw_transpose(k + 1)
                if has(k - 1, 0, NT):
                    router(k - 1)
                if has(k, 0, NT):
                    values(k, par)
                    o_transpose(k)
                    out_project(k)

            half_reg = [None]

            def half_of(k, par):
                if isinstance(k, int):
                    return (k + 1) // 2
                return half_reg[0] + par

            pe.wait_ge(w_in, ALL_IN)
            for k in range(-1, 2):
                step(k, k % 2)
            with pe.Fori(1, NT // 2 - 1) as i:
                half_reg[0] = i
                step(i * 2, 0)
                step(i * 2 + 1, 1)
            for k in range(NT - 2, NT + 1):
                step(k, k % 2)

        @block.scalar
        def _(act):
            act.wait_ge(w_in, ALL_IN)
            nc.scalar.preload_act_table_set("natural_log_exp_and_others")
            nc.scalar.activation(expb[:], small[:, 4:6], ACT.Exp, scale=-1.0).then_inc(c_ok, 1)

            def step(k, par):
                nxt = 1 - par
                if has(k, 0, NT):
                    ge(act, s["norm_mm"], k + 1)
                    nc.scalar.activation(ln[:], X, ACT.Ln).then_inc(s["ln_ok"], 1)
                    ge(act, s["ln_ok"], k + 1)
                    ge(act, s["w_ok"], k)
                    nc.scalar.activation(rn[:], ln[:], ACT.Exp, scale=-1.0).then_inc(s["rn_ok"], 1)
                if has(k - 1, 0, NT):
                    ge(act, s["x2_tr"], k)
                    ge(act, s["x2Tc_ok"], k - 1)
                    ge(act, s["lg_mm"], k - 1)
                    nc.scalar.activation(x2T[:], pX2T, ACT.Copy).then_inc(s["x2T_ok"], 1)
                if has(k, -1, NT - 1):
                    ge(act, s["x1_tr"], k + 2)
                    ge(act, s["v_mm"], k + 1)
                    nc.scalar.activation(x1T[:], pX1T, ACT.Copy).then_inc(s["x1T_ok"], 1)
                if has(k, 0, NT):
                    ge(act, s["scd_ok"], k + 1)
                    ge(act, s["w_ok"], k)
                    nc.scalar.activation(ex[:], scd[:, :, :].rearrange("p h c -> p (h c)"), ACT.Exp)\
                        .then_inc(s["e_ok"], 1)
                if has(k, -1, NT - 1):
                    ge(act, s["cwd_ok"], k + 2)
                    ge(act, s["ab_mm"], k)
                    nc.scalar.activation(cwT[:, nxt], cwd[:], ACT.Exp).then_inc(s["cwT_ok"], 1)
                if has(k, 0, NT):
                    ge(act, s["w_tr"], k + 1)
                    ge(act, s["ab_mm"], k)
                    nc.scalar.activation(wT[:], Z, ACT.Copy).then_inc(s["wT_ok"], 1)
                if has(k, -1, NT - 1):
                    ge(act, s["cw_tr"], k + 2)
                    ge(act, s["s_mm"], k + 1)
                    nc.scalar.activation(cw[:], Z, ACT.Copy).then_inc(s["cw_ok"], 1)
                if has(k, 0, NT):
                    ge(act, s["o_tr"], k + 1)
                    ge(act, s["y_mm"], k)
                    nc.scalar.activation(oT[:], pOT, ACT.Copy).then_inc(s["oT_ok"], 1)

            steps(act, step, -1, NT + 1)

        @block.gpsimd
        def _(pool):
            nc.gpsimd.memset(mhalf[:], -0.5).then_inc(c_ok, 1)
            nc.gpsimd.memset(keep["zeros"][:], 0.0).then_inc(z_ok, 1)
            pool.wait_ge(c_ok, 2)

            def rsqrt(t, n, ve, r):
                ge(pool, s[f"ve{n}_ok"], t + 1)
                nc.gpsimd.tensor_tensor(r[:], ve[:], mhalf[:], ALU.pow).then_inc(s[f"r{n}_ok"], 1)

            def step(k, par):
                if has(k - 1, 0, NT):
                    rsqrt(k - 1, 2, ve2, r2)
                if has(k, -1, NT - 1):
                    rsqrt(k + 1, 0, ve0, r0)
                    rsqrt(k + 1, 1, ve1, r1)
                if has(k - 1, 0, NT):
                    ge(pool, s["x2_ok"], k)
                    nc.gpsimd.tensor_copy(x2_all[:, k - 1, :], x2[:]).then_inc(s["x2c_ok"], 1)
                    nc.gpsimd.tensor_copy(h2_all[:, k - 1, :], h2[:]).then_inc(s["h2c_ok"], 1)
                    ge(pool, s["x2T_ok"], k)
                    nc.gpsimd.tensor_copy(x2T_all[:, k - 1, :, :], x2T[:]).then_inc(s["x2Tc_ok"], 1)
                if has(k, 0, NT):
                    ge(pool, s["e_ok"], k + 1)
                    ge(pool, s["w_tr"], k)
                    nc.gpsimd.tensor_tensor(w[:, :, :].rearrange("p j c -> p (j c)"), ex[:], rn[:], ALU.mult)\
                        .then_inc(s["w_ok"], 1)

            steps(pool, step, -1, NT + 1)

        @block.vector
        def _(dve):
            dve.wait_ge(w_in, ALL_IN)
            nc.vector.memset(v1[:, :, :, DH:VW], 1.0).then_inc(c_ok, 1)
            dve.wait_ge(c_ok, 3)
            for c in range(KD):
                for e in range(2):
                    last = nc.vector.tensor_scalar(qscale[:, c, e:e + 1], small[:, 6 + e:7 + e], expb[:, c:c + 1],
                                                   DH ** -0.5, ALU.mult, ALU.mult)
            last.then_inc(c_ok, 1)
            dve.wait_ge(c_ok, 4)

            def stats(t, n, src, st, mv, ve):
                nc.vector.bn_stats(st[:], src).then_inc(s[f"st{n}_ok"], 1)
                ge(dve, s[f"st{n}_ok"], t + 1)
                nc.vector.tensor_copy(touch[:], st[:, 0:1])
                nc.vector.bn_aggr(mv[:], st[:]).then_inc(s[f"mv{n}_ok"], 1)
                ge(dve, s[f"mv{n}_ok"], t + 1)
                ge(dve, s[f"r{n}_ok"], t)
                nc.vector.tensor_scalar(ve[:], mv[:, 1:2], EPS, None, ALU.add).then_inc(s[f"ve{n}_ok"], 1)

            def masked(src, dst, done):
                nc.vector.tensor_tensor(dst, src.rearrange("p (j n) -> p j n", j=HP),
                                        mask[:, :].unsqueeze(1).broadcast_to([P, HP, P]), ALU.mult).then_inc(s[done], 1)

            def step(k, par):
                nxt = 1 - par
                if has(k - 1, 0, NT):
                    ge(dve, s["y_mm"], k)
                    nc.vector.tensor_tensor(yb[:], pY, bo[:], ALU.add).then_inc(s["yb_ok"], 1)
                    ge(dve, s["yb_ok"], k)
                    ge(dve, s["h2c_ok"], k - 1)
                    nc.vector.tensor_tensor(h2[:], yb[:], h1[:, nxt, :], ALU.add).then_inc(s["h2_ok"], 1)
                    ge(dve, s["h2_ok"], k)
                    stats(k - 1, 2, h2[:], st2, mv2, ve2)
                if has(k, -1, NT - 1):
                    ge(dve, s["tok_mm"], k + 2)
                    stats(k + 1, 0, pTok, st0, mv0, ve0)
                if has(k - 1, 0, NT):
                    ge(dve, s["r2_ok"], k)
                    ge(dve, s["x2c_ok"], k - 1)
                    ge(dve, s["x2_tr"], k - 1)
                    nc.vector.tensor_scalar(x2[:], h2[:], mv2[:, 0:1], r2[:], ALU.subtract, ALU.mult)\
                        .then_inc(s["x2_ok"], 1)
                if has(k, -1, NT - 1):
                    ge(dve, s["r0_ok"], k + 2)
                    nc.vector.tensor_scalar(h0[:], pTok, mv0[:, 0:1], r0[:], ALU.subtract, ALU.mult)\
                        .then_inc(s["h0_ok"], 1)
                    ge(dve, s["h0_ok"], k + 2)
                    nc.vector.tensor_tensor(h1[:, nxt, :], h0[:], gamma[:], ALU.mult).then_inc(s["h1_ok"], 1)
                    ge(dve, s["h1_ok"], k + 2)
                    stats(k + 1, 1, h1[:, nxt, :], st1, mv1, ve1)
                if has(k, 0, NT):
                    ge(dve, s["s_mm"], k + 1)
                    ge(dve, s["rn_ok"], k + 1)
                    nc.vector.tensor_tensor(sc[:, :, :].rearrange("p h c -> p (h c)"), Y, rn[:], ALU.mult)\
                        .then_inc(s["sc_ok"], 1)
                if has(k, -1, NT - 1):
                    ge(dve, s["r1_ok"], k + 2)
                    ge(dve, s["x1_tr"], k + 1)
                    nc.vector.tensor_scalar(x1[:], h1[:, nxt, :], mv1[:, 0:1], r1[:], ALU.subtract, ALU.mult)\
                        .then_inc(s["x1_ok"], 1)
                if has(k, 0, NT):
                    ge(dve, s["sc_ok"], k + 1)
                    nc.vector.tensor_reduce(scm[:], sc[:], AX.X, ALU.max).then_inc(s["scm_ok"], 1)
                    ge(dve, s["scm_ok"], k + 1)
                    ge(dve, s["e_ok"], k)
                    nc.vector.tensor_tensor(scd[:], sc[:], bc(scm[:, :], [P, H, C]), ALU.subtract)\
                        .then_inc(s["scd_ok"], 1)
                if has(k, -1, NT - 1):
                    ge(dve, s["qk_mm"], k + 2)
                    ge(dve, s["qkb_mm"], k + 1)
                    for c in range(KD):
                        for e in range(2):
                            last = nc.vector.tensor_scalar(qz[:, c, e, :], pQK[:, c * P:(c + 1) * P], small[:, c:c + 1],
                                                           qscale[:, c, e:e + 1], ALU.add, ALU.mult)
                    last.then_inc(s["qz_ok"], 1)
                    ge(dve, s["cwT_mm"], k + 1)
                    for c in range(KD):
                        last = nc.vector.tensor_scalar(kT[:, c, :], pQK[:, (2 + c) * P:(3 + c) * P],
                                                       small[:, 2 + c:3 + c], None, ALU.add)
                    last.then_inc(s["kT_ok"], 1)
                    ge(dve, s["v_mm"], k + 2)
                    ge(dve, s["o_mm"], k)
                    nc.vector.tensor_tensor(v1[:, nxt, :, 0:DH], pV.rearrange("p (h d) -> p h d", h=H),
                                            bv[:, :].rearrange("p (h d) -> p h d", h=H), ALU.add).then_inc(s["v_ok"], 1)
                    ge(dve, s["s_mm"], k + 1)
                    ge(dve, s["qka_mm"], k + 2)
                    masked(Z, qkm[:, 0], "qkma_ok")
                    ge(dve, s["qkb_mm"], k + 2)
                    masked(X, qkm[:, 1], "qkmb_ok")
                    ge(dve, s["cwT_mm"], k + 2)
                    nc.vector.tensor_reduce(mx[:], Y.rearrange("p (n s) -> p n s", s=S), AX.X, ALU.max)\
                        .then_inc(s["mx_ok"], 1)
                    ge(dve, s["mx_ok"], k + 2)
                    ge(dve, s["cwT_ok"], k + 1)
                    nc.vector.tensor_tensor(cwd[:, :, :].rearrange("p j (n s) -> p (j n) s", s=S),
                                            Y.rearrange("p (n s) -> p n s", s=S), bc(mx[:, :], [P, P, S]), ALU.subtract)\
                        .then_inc(s["cwd_ok"], 1)
                if has(k, 0, NT):
                    ge(dve, s["o_mm"], k)
                    ge(dve, s["aa_mm"], k + 1)
                    masked(X, am[:, 0], "ama_ok")
                    ge(dve, s["ab_mm"], k + 1)
                    masked(Y, am[:, 1], "amb_ok")
                if has(k - 1, 0, NT):
                    ge(dve, s["lg_mm"], k)
                    nc.vector.tensor_copy(lg_all[:, k - 1, :], pLg).then_inc(s["lg_ok"], 1)
                if has(k, 0, NT):
                    ge(dve, s["o_mm"], k + 1)
                    pOh = pO.rearrange("p (h d) -> p h d", h=H)
                    nc.vector.reciprocal(rz[:], pOh[:, :, DH]).then_inc(s["rz_ok"], 1)
                    ge(dve, s["rz_ok"], k + 1)
                    ge(dve, s["o_tr"], k)
                    nc.vector.tensor_tensor(on[:], pOh[:, :, 0:DH], bc(rz[:, :], [P, H, DH]), ALU.mult)\
                        .then_inc(s["on_ok"], 1)

            steps(dve, step, -1, NT + 1)


def gated_unit_buffers(nc, ctx, tag, ps):

    def sb(name, shape, dt=F32):
        return ctx.enter_context(nc.sbuf_tensor(tag + name, shape, dt))

    u = {
        "xT": sb("xT", [P, 2, KD, P]), "sil": sb("sil", [P, 2, HE]), "h": sb("h", [P, 2, HE]),
        "hT": sb("hT", [P, KH, P]),
        "gate": [ps[:, 0:HE], ps[:, 512:512 + HE]], "up": [ps[:, 1024:1024 + HE], ps[:, 1536:1536 + HE]],
        "pHT": ps[:, 2048:2048 + KH * P], "y": [ps[:, 2560:2560 + D], ps[:, 3072:3072 + D]],
        "pXT": ps[:, 3584:3584 + KD * P],
    }
    for n in "gate_mm up_mm h_tr y_mm xT_ok sil_ok h_ok hT_ok y_ok".split():
        u[n] = ctx.enter_context(nc.semaphore(tag + n))
    return u


def tensor_gate(nc, pe, u, n, par, w):
    ge(pe, u["xT_ok"], n + 1)
    ge(pe, u["sil_ok"], n - 1)
    for c in range(KD):
        last = nc.tensor.matmul(u["gate"][par], u["xT"][:, par, c, :], w(c)[0], start=c == 0, stop=c == KD - 1)
    last.then_inc(u["gate_mm"], 1)


def tensor_up(nc, pe, u, n, par, w):
    ge(pe, u["h_ok"], n - 1)
    for c in range(KD):
        last = nc.tensor.matmul(u["up"][par], u["xT"][:, par, c, :], w(c)[1], start=c == 0, stop=c == KD - 1)
    last.then_inc(u["up_mm"], 1)


def tensor_transpose_h(nc, pe, u, n, par, ident):
    ge(pe, u["h_ok"], n + 1)
    ge(pe, u["hT_ok"], n)
    for c in range(KH):
        last = nc.tensor.transpose(u["pHT"][0:HK[c], c * P:(c + 1) * P], u["h"][:, par, c * P:c * P + HK[c]], ident[:])
    last.then_inc(u["h_tr"], 1)


def tensor_down(nc, pe, u, n, par, w3):
    ge(pe, u["hT_ok"], n + 1)
    ge(pe, u["y_ok"], n - 1)
    for c in range(KH):
        last = nc.tensor.matmul(u["y"][par], u["hT"][0:HK[c], c, :], w3(c), start=c == 0, stop=c == KH - 1)
    last.then_inc(u["y_mm"], 1)


def scalar_silu(nc, act, u, n, par):
    ge(act, u["gate_mm"], n + 1)
    ge(act, u["h_ok"], n - 1)
    nc.scalar.activation(u["sil"][:, par, :], u["gate"][par], ACT.Silu).then_inc(u["sil_ok"], 1)


def scalar_hT(nc, act, u, n):
    ge(act, u["h_tr"], n + 1)
    ge(act, u["y_mm"], n)
    nc.scalar.activation(u["hT"][:, 0:KH - 1, :], u["pHT"][:, 0:(KH - 1) * P], ACT.Copy)
    nc.scalar.activation(u["hT"][0:HK[-1], KH - 1, :], u["pHT"][0:HK[-1], (KH - 1) * P:KH * P], ACT.Copy)\
        .then_inc(u["hT_ok"], 1)


def vector_h(nc, dve, u, n, par):
    ge(dve, u["up_mm"], n + 1)
    ge(dve, u["sil_ok"], n + 1)
    ge(dve, u["h_tr"], n - 1)
    nc.vector.tensor_tensor(u["h"][:, par, :], u["sil"][:, par, :], u["up"][par], ALU.mult).then_inc(u["h_ok"], 1)


def pairs(eng, body, count):
    for k in range(-1, 2):
        body(k, k % 2)
    loops = (count - 3) // 2
    with eng.Fori(1, 1 + loops) as i:
        body(i * 2, 0)
        body(i * 2 + 1, 1)
    for k in range(2 + 2 * loops, count):
        body(k, k % 2)


def shared_stage(nc, ctx, io, keep):

    def sb(name, shape, dt=F32):
        return ctx.enter_context(nc.sbuf_tensor(name, shape, dt))

    def sem(name):
        return ctx.enter_context(nc.semaphore(name))

    ident, x2_all, x2T_all, lg_all, h2_all, ps = (keep[n] for n in ("ident", "x2", "x2T", "lg", "h2", "ps"))
    slots, prob, tile_expert = keep["slots"], keep["prob"], keep["tile_expert"]
    ws12, ws3 = keep["ws12"], keep["ws3"]

    u = gated_unit_buffers(nc, ctx, "sh_", ps)
    strict, ones = sb("strict", [P, P]), sb("ones", [P, P])
    rc = sb("rc", [P, RC])
    thr, rev, tile_no = rc[:, 0:NT], rc[:, NT:NT + E], rc[:, NT + E:RC]
    names = """lga rank oneh1 oneh2 lgb rankb oneh picked tot grid gsel""".split()
    b = {n: sb("r_" + n, [P, E, NT]) for n in names}
    m1, m2, f1, f2, dm = (sb("r_" + n, [P, NT]) for n in "m1 m2 f1 f2 dm".split())
    cum, ones_row = sb("cum", [P, E * NT]), sb("ones_row", [P, E * NT])
    cmp16, cnt, nt, ntI, base, off = (sb("r_" + n, [P, E, NT] if n == "cmp16" else [P, E])
                                      for n in "cmp16 cnt nt ntI base off".split())
    tcmp, tex = sb("tcmp", [P, NS, E]), sb("tex", [P, NS])
    slotf = sb("slotf", [P, 2, NT])

    r_in, r_ok, r_mm, r_e = sem("B_r_in"), sem("B_r_ok"), sem("B_r_mm"), sem("B_r_e")
    slot_ok, sent = sem("B_slot_ok"), sem("B_sent")
    pR, pTot = ps[:, 2560:2560 + P], ps[:, 3072:3072 + P]

    UN = 2 * NT

    with nc.Block() as block:

        @block.sync
        def _(sp):
            for dst, src in ((strict, io["strict"]), (ones, io["ones"]), (rc, io["rc"])):
                sp.dma_start(dst[:], src).then_inc(r_in, 16)

        @block.tensor
        def _(pe):
            pe.wait_ge(r_in, 48)
            pe.wait_ge(r_ok, ONEHOT)
            onehot = b["oneh"][:, :, :].rearrange("p e t -> p (e t)")
            nc.tensor.matmul(pR, strict[:], onehot, start=True, stop=True)
            nc.tensor.matmul(pTot, ones[:], onehot, start=True, stop=True).then_inc(r_mm, 1)
            pe.wait_ge(slot_ok, 1)

            def step(k, par):
                w = lambda c: (ws12[:, 1 - par, c, 0:HE], ws12[:, 1 - par, c, HE:2 * HE])
                if has(k, -1, UN - 1):
                    tensor_gate(nc, pe, u, k + 1, 1 - par, w)
                if has(k, 0, UN):
                    tensor_transpose_h(nc, pe, u, k, par, ident)
                if has(k, -1, UN - 1):
                    tensor_up(nc, pe, u, k + 1, 1 - par, w)
                if has(k, 0, UN):
                    tensor_down(nc, pe, u, k, par, lambda c: ws3[0:HK[c], par, c, :])

            pairs(pe, step, UN)

        @block.scalar
        def _(act):
            act.wait_ge(r_ok, DIFF)
            nc.scalar.activation(f2[:], dm[:], ACT.Exp).then_inc(r_e, 1)

            def step(k, par):
                if has(k, -1, UN - 1):
                    t = (k + 1) // 2 if isinstance(k, int) else None
                    ge(act, u["up_mm"], k)
                    src = x2T_all[:, t, :, :] if t is not None else x2T_all[:, tile_of[0] + par, :, :]
                    nc.scalar.activation(u["xT"][:, 1 - par], src, ACT.Copy).then_inc(u["xT_ok"], 1)
                    scalar_silu(nc, act, u, k + 1, 1 - par)
                if has(k, 0, UN):
                    scalar_hT(nc, act, u, k)

            tile_of = [None]
            for k in range(-1, 2):
                step(k, k % 2)
            loops = (UN - 3) // 2
            with act.Fori(1, 1 + loops) as i:
                tile_of[0] = i
                step(i * 2, 0)
                step(i * 2 + 1, 1)
            for k in range(2 + 2 * loops, UN):
                step(k, k % 2)

        @block.vector
        def _(dve):
            v = nc.vector
            done = [0]

            def link(ins):
                done[0] += 1
                ins.then_inc(r_ok, 1)
                dve.wait_ge(r_ok, done[0])

            def over_e(ap):
                return ap.rearrange("p e t -> p t e")

            def each_e(ap):
                return ap.unsqueeze(1).broadcast_to([P, E, NT])

            def first_of(logits, m, eq, rank, fi, onehot):
                link(v.tensor_reduce(m[:], over_e(logits), AX.X, ALU.max))
                link(v.tensor_tensor(eq[:], logits, each_e(m[:, :]), ALU.is_equal))
                link(v.tensor_tensor(rank[:], eq[:], bc(rev, [P, E, NT]), ALU.mult))
                link(v.tensor_reduce(fi[:], over_e(rank[:, :, :]), AX.X, ALU.max))
                link(v.tensor_tensor(onehot[:], bc(rev, [P, E, NT]), each_e(fi[:, :]), ALU.is_equal))

            dve.wait_ge(r_in, 48)
            link(v.tensor_copy(b["lga"][:], lg_all[:, :, :].rearrange("p t e -> p e t")))
            first_of(b["lga"][:, :, :], m1, b["gsel"], b["rank"], f1, b["oneh1"])
            link(v.scalar_tensor_tensor(b["lgb"][:, :, :].rearrange("p e t -> p (e t)"),
                                        b["oneh1"][:, :, :].rearrange("p e t -> p (e t)"), -1e30,
                                        b["lga"][:, :, :].rearrange("p e t -> p (e t)"), ALU.mult, ALU.add))
            first_of(b["lgb"][:, :, :], m2, b["picked"], b["rankb"], f1, b["oneh2"])
            link(v.tensor_tensor(b["oneh"][:], b["oneh1"][:], b["oneh2"][:], ALU.add))
            assert done[0] == ONEHOT
            link(v.tensor_tensor(dm[:], m2[:], m1[:], ALU.subtract))
            assert done[0] == DIFF
            link(v.memset(ones_row[:], 1.0))
            dve.wait_ge(r_mm, 1)
            link(v.tensor_copy(b["tot"][:, :, :].rearrange("p e t -> p (e t)"), pTot))
            link(v.tensor_tensor_scan(cum[:], ones_row[:], b["tot"][:, :, :].rearrange("p e t -> p (e t)"), 0.0,
                                      ALU.mult, ALU.add))
            link(v.tensor_reduce(cnt[:], b["tot"][:], AX.X, ALU.add))
            link(v.tensor_tensor(cmp16[:], bc(cnt[:, :], [P, E, NT]), each_e(thr), ALU.is_gt))
            link(v.tensor_reduce(nt[:], cmp16[:], AX.X, ALU.add))
            link(v.tensor_tensor_scan(ntI[:], ones_row[:, 0:E], nt[:], 0.0, ALU.mult, ALU.add))
            link(v.tensor_tensor(base[:], ntI[:], nt[:], ALU.subtract))
            link(v.tensor_tensor(off[:], cum[:, :].rearrange("p (e t) -> p e t", t=NT)[:, :, NT - 1], cnt[:], ALU.subtract))
            link(v.scalar_tensor_tensor(off[:], base[:], float(P), off[:], ALU.mult, ALU.subtract))
            link(v.tensor_tensor(b["grid"][:, :, :].rearrange("p e t -> p (e t)"), pR, cum[:], ALU.add))
            link(v.tensor_tensor(b["grid"][:], b["grid"][:], b["tot"][:], ALU.subtract))
            link(v.tensor_tensor(b["grid"][:], b["grid"][:], bc(off[:, :], [P, E, NT]), ALU.add))
            for n in range(2):
                link(v.tensor_tensor(b["gsel"][:], b["grid"][:], b[f"oneh{n + 1}"][:], ALU.mult))
                link(v.tensor_reduce(slotf[:, n, :], over_e(b["gsel"][:, :, :]), AX.X, ALU.add))
            link(v.tensor_copy(slots[:], slotf[:]))
            link(v.tensor_tensor(tcmp[:], bc(tile_no, [P, NS, E]), ntI[:, :].unsqueeze(1).broadcast_to([P, NS, E]),
                                 ALU.is_ge))
            link(v.tensor_reduce(tex[:], tcmp[:], AX.X, ALU.add))
            link(v.tensor_scalar(tile_expert[:], tex[:], float(E - 1), None, ALU.min))
            dve.wait_ge(r_e, 1)
            link(v.tensor_scalar(m1[:], f2[:], 1.0, None, ALU.add))
            link(v.reciprocal(prob[:, 0, :], m1[:]))
            link(v.tensor_tensor(prob[:, 1, :], prob[:, 0, :], f2[:], ALU.mult))
            v.memset(dm[:], 0.0).then_inc(slot_ok, 1)

            def step(k, par):
                if has(k, -1, UN - 1):
                    vector_h(nc, dve, u, k + 1, 1 - par)
                if has(k, 0, UN):
                    t = k // 2 if isinstance(k, int) else tile_of[0]
                    ge(dve, u["y_mm"], k + 1)
                    ge(dve, u["y_ok"], k)
                    v.tensor_tensor(h2_all[:, t, :], h2_all[:, t, :], u["y"][par], ALU.add).then_inc(u["y_ok"], 1)

            tile_of = [None]
            for k in range(-1, 2):
                step(k, k % 2)
            loops = (UN - 3) // 2
            with dve.Fori(1, 1 + loops) as i:
                tile_of[0] = i
                step(i * 2, 0)
                step(i * 2 + 1, 1)
            for k in range(2 + 2 * loops, UN):
                step(k, k % 2)

        @block.gpsimd
        def _(pool):
            pool.wait_ge(slot_ok, 1)
            pool.wait_ge(keep["xs_zero"], 16)
            for t in range(NT):
                for n in range(2):
                    nc.gpsimd.indirect_dma_start(
                        out=keep["xs"], out_offset=bass.IndirectOffsetOnAxis(ap=slots[:, n, t:t + 1], axis=0),
                        in_=x2_all[:, t, :], in_offset=None).then_inc(sent, 16)
            pool.wait_ge(sent, 16 * 2 * NT)


def routed_stage(nc, ctx, io, keep):

    def sb(name, shape, dt=F32):
        return ctx.enter_context(nc.sbuf_tensor(name, shape, dt))

    def sem(name):
        return ctx.enter_context(nc.semaphore(name))

    ident, ps, tile_expert = keep["ident"], keep["ps"], keep["tile_expert"]
    w12, w3 = keep["w12"], keep["w3"]
    u = gated_unit_buffers(nc, ctx, "ro_", ps)
    xr = sb("xr", [P, 2, D])
    yo = sb("yo", [P, 2, D])
    xr_in = [sem("C_xr_in0"), sem("C_xr_in1")]
    y_out = [sem("C_y_out0"), sem("C_y_out1")]
    x_tr = sem("C_x_tr")
    xs = keep["xs"].rearrange("(j p) d -> j p d", p=P)
    ys = keep["ys"].rearrange("(j p) d -> j p d", p=P)

    with nc.Block() as block:

        def run(eng, body):
            for k in range(-2, 2):
                body(k, k % 2, k // 2)
            loops = (NS - 4) // 2
            with eng.Fori(1, 1 + loops) as i:
                body(i * 2, 0, i)
                body(i * 2 + 1, 1, i)
            for k in range(2 + 2 * loops, NS):
                body(k, k % 2, k // 2)

        @block.sync
        def _(sp):
            def step(k, par, i):
                if has(k, -2, NS - 2):
                    ge(sp, x_tr, k + 1)
                    sp.dma_start(xr[:, par, :], xs[k + 2]).then_inc(xr_in[par], 16)
                if has(k, 0, NS):
                    ge(sp, u["y_ok"], k + 1)
                    sp.dma_start(ys[k], yo[:, par, :]).then_inc(y_out[par], 16)

            run(sp, step)
            sp.wait_ge(y_out[0], 16 * ((NS + 1) // 2))
            sp.wait_ge(y_out[1], 16 * (NS // 2))

        @block.tensor
        def _(pe):
            pe.wait_ge(keep["w_in"], 32)

            def expert(k):
                return pe.value_load(tile_expert[0:1, k:k + 1] if isinstance(k, int) else
                                     tile_expert[0:1, bass.ds(k, 1)], min_val=0, max_val=E - 1)

            e_of = {}

            def step(k, par, i):
                if has(k, -2, NS - 2):
                    ge(pe, xr_in[par], 16 * (i + 2))
                    ge(pe, u["xT_ok"], k + 2)
                    for c in range(KD):
                        last = nc.tensor.transpose(u["pXT"][:, c * P:(c + 1) * P], xr[:, par, c * P:(c + 1) * P], ident[:])
                    last.then_inc(x_tr, 1)
                if has(k, -1, NS - 1):
                    e = expert(k + 1)
                    e_of[1 - par] = e
                    w = lambda c: (w12[:, e, c, 0:HE], w12[:, e, c, HE:2 * HE])
                    tensor_gate(nc, pe, u, k + 1, 1 - par, w)
                if has(k, 0, NS):
                    tensor_transpose_h(nc, pe, u, k, par, ident)
                if has(k, -1, NS - 1):
                    tensor_up(nc, pe, u, k + 1, 1 - par, w)
                if has(k, 0, NS):
                    e2 = expert(k)
                    tensor_down(nc, pe, u, k, par, lambda c: w3[0:HK[c], e2, c, :])

            run(pe, step)

        @block.scalar
        def _(act):
            def step(k, par, i):
                if has(k, -2, NS - 2):
                    ge(act, x_tr, k + 3)
                    ge(act, u["up_mm"], k + 1)
                    nc.scalar.activation(u["xT"][:, par], u["pXT"], ACT.Copy).then_inc(u["xT_ok"], 1)
                if has(k, -1, NS - 1):
                    scalar_silu(nc, act, u, k + 1, 1 - par)
                if has(k, 0, NS):
                    scalar_hT(nc, act, u, k)

            run(act, step)

        @block.vector
        def _(dve):
            def step(k, par, i):
                if has(k, -1, NS - 1):
                    vector_h(nc, dve, u, k + 1, 1 - par)
                if has(k, 0, NS):
                    ge(dve, u["y_mm"], k + 1)
                    ge(dve, y_out[par], 16 * i)
                    nc.vector.tensor_copy(yo[:, par, :], u["y"][par]).then_inc(u["y_ok"], 1)

            run(dve, step)


def final_stage(nc, ctx, io, keep):

    def sb(name, shape, dt=F32):
        return ctx.enter_context(nc.sbuf_tensor(name, shape, dt))

    def sem(name):
        return ctx.enter_context(nc.semaphore(name))

    ident, ps, h2_all, slots, prob = (keep[n] for n in ("ident", "ps", "h2", "slots", "prob"))
    R = N // P
    gat = sb("gat", [P, 2, 2, D])
    h3a = sb("h3a", [P, NT, D])
    h3b = sb("h3b", [P, NT, D])
    wT, a1, a2, wc = (sb("L_" + n, [P, KD, D]) for n in ("wT", "a1", "a2", "wc"))
    ut = sb("ut", [P, KD, D])
    bias = sb("bias", [P, D])
    ones, mhalf, touch = sb("L_ones", [P, P]), sb("L_mhalf", [P, R]), sb("L_touch", [P, 1])
    gath = [sem("D_gath0"), sem("D_gath1")]
    ha_ok, hb_ok, h_out, w_in, wc_ok, wc_mm, c_ok = (sem("D_" + n) for n in
        "ha_ok hb_ok h_out w_in wc_ok wc_mm c_ok".split())

    with nc.Block() as block:

        @block.sync
        def _(sp):
            for dst, src in ((wT, io["l1w"]), (a1, io["l1a1"]), (a2, io["l1a2"]),
                             (bias, io["l1b"].partition_broadcast(P)), (ones, io["ones"])):
                sp.dma_start(dst[:], src).then_inc(w_in, 16)
            hb = keep["hb"].rearrange("s (t n) d -> t n s d", t=NT)
            with sp.Fori(0, NT) as t:
                sp.wait_ge(hb_ok, t + 1)
                sp.dma_start(hb[t], h3b[:, t, :]).then_inc(h_out, 16)
            sp.wait_ge(h_out, 16 * NT)
            sp.wait_ge(w_in, 80)

        @block.gpsimd
        def _(pool):
            nc.gpsimd.memset(mhalf[:], -0.5).then_inc(c_ok, 1)
            for t in range(NT):
                ge(pool, hb_ok, t - 1)
                for n in range(2):
                    nc.gpsimd.indirect_dma_start(
                        out=gat[:, t % 2, n, :], out_offset=None, in_=keep["ys"],
                        in_offset=bass.IndirectOffsetOnAxis(ap=slots[:, n, t:t + 1], axis=0)).then_inc(gath[t % 2], 16)

        @block.vector
        def _(dve):
            def tile(t, par, i):
                ge(dve, gath[par], 32 * (i + 1))
                nc.vector.scalar_tensor_tensor(h3a[:, t, :], gat[:, par, 0, :], prob[:, 0, t:t + 1] if isinstance(t, int)
                                               else prob[:, 0, bass.ds(t, 1)], h2_all[:, t, :], ALU.mult, ALU.add)\
                    .then_inc(ha_ok, 1)
                ge(dve, ha_ok, t + 1)
                nc.vector.scalar_tensor_tensor(h3b[:, t, :], gat[:, par, 1, :], prob[:, 1, t:t + 1] if isinstance(t, int)
                                               else prob[:, 1, bass.ds(t, 1)], h3a[:, t, :], ALU.mult, ALU.add)\
                    .then_inc(hb_ok, 1)

            with dve.Fori(0, NT // 2) as i:
                tile(i * 2, 0, i)
                tile(i * 2 + 1, 1, i)
            dve.wait_ge(wc_mm, 1)
            nc.vector.tensor_copy(ut[:], ps[:, 0:2 * D]).then_inc(wc_ok, 1)
            dve.wait_ge(wc_mm, 2)
            nc.vector.tensor_copy(wc[:], ps[:, 512:512 + 2 * D]).then_inc(wc_ok, 1)

        @block.tensor
        def _(pe):
            pe.wait_ge(w_in, 80)
            for m in range(KD):
                for c in range(KD):
                    last = nc.tensor.matmul(ps[:, m * D:(m + 1) * D], a1[:, c, m * P:(m + 1) * P], wT[:, c, :],
                                            start=c == 0, stop=c == KD - 1)
            last.then_inc(wc_mm, 1)
            pe.wait_ge(wc_ok, 1)
            for m in range(KD):
                for c in range(KD):
                    last = nc.tensor.matmul(ps[:, 512 + m * D:512 + (m + 1) * D], ut[:, c, m * P:(m + 1) * P],
                                            a2[:, c, :], start=c == 0, stop=c == KD - 1)
            last.then_inc(wc_mm, 1)

    hin = sb("hin", [P, 2, R, D])
    st3, mv3, ve3, r3 = sb("st3", [P, R, 6]), sb("mv3", [P, R, 2]), sb("ve3", [P, R]), sb("r3", [P, R])
    st4, mv4, ve4, r4 = sb("st4", [P, R, 6]), sb("mv4", [P, R, 2]), sb("ve4", [P, R]), sb("r4", [P, R])
    x3 = sb("x3", [P, 2, R, D])
    sq, ss, ssc, rin = sb("sq", [P, R, D]), sb("ss", [P, R]), sb("ssc", [P, R]), sb("rin", [P, R])
    diag = sb("diag", [P, R, P])
    x3T = sb("x3T", [P, KD, N])
    fac = sb("fac", [P, R, N])
    sim = sb("sim", [P, R, N])
    nm = sb("nm", [P, R])
    pr = sb("pr", [P, R, N])
    sm, rs = sb("sm", [P, R]), sb("rs", [P, 2, R])
    pT = sb("pT", [P, R, N])
    av = sb("av", [P, R, D])
    h4 = sb("h4", [P, 2, R, D])
    x4 = sb("x4", [P, R, D])
    x4T = sb("x4T", [P, KD, N])
    yb = sb("L_yb", [P, R, D])
    th = sb("th", [P, R, D])
    ho = sb("ho", [P, 2, R, D])
    pT3, pRow, pDot, pPT, pAV, pT4, pY = (ps[:, 512 * n:512 * (n + 1)] for n in range(7))
    names = """x3_tr row_mm dot_mm p_tr av_mm x4_tr y_mm  x3T_ok p_ok pT_ok x4T_ok th_ok
        st3_ok mv3_ok ve3_ok r3_ok x3_ok sq_ok ss_ok ssc_ok rin_ok diag_ok fac_ok sim_ok nm_ok rs_ok av_ok h4_ok
        st4_ok mv4_ok ve4_ok r4_ok x4_ok yb_ok ho_ok""".split()
    s = {n: sem("E_" + n) for n in names}
    h_in, o_out = [sem("E_h_in0"), sem("E_h_in1")], [sem("E_o_out0"), sem("E_o_out1")]

    with nc.Block() as block:

        def run(eng, body):
            for k in range(-1, 2):
                body(k, k % 2, k // 2)
            with eng.Fori(1, S // 2 - 1) as i:
                body(i * 2, 0, i)
                body(i * 2 + 1, 1, i)
            for k in range(S - 2, S + 1):
                body(k, k % 2, k // 2)

        hb = keep["hb"].rearrange("s (r p) d -> s p r d", p=P)
        ob = io["out"].rearrange("s (r p) d -> s p r d", p=P)

        @block.sync
        def _(sp):
            sp.dma_start(hin[:, 0], hb[0]).then_inc(h_in[0], 16)

            def step(k, par, i):
                if has(k, -1, S - 2):
                    ge(sp, s["h4_ok"], k + 1)
                    sp.dma_start(hin[:, par], hb[k + 2]).then_inc(h_in[par], 16)
                if has(k, 1, S + 1):
                    ge(sp, s["ho_ok"], k)
                    sp.dma_start(ob[k - 1], ho[:, 1 - par]).then_inc(o_out[1 - par], 16)

            run(sp, step)
            for par in range(2):
                sp.wait_ge(o_out[par], 16 * (S // 2))

        @block.tensor
        def _(pe):
            mm, tr = nc.tensor.matmul, nc.tensor.transpose

            def transposes(out, src):
                for c in range(KD):
                    for r in range(R):
                        last = tr(out[:, c * N + r * P:c * N + (r + 1) * P], src[:, r, c * P:(c + 1) * P], ident[:])
                return last

            def step(k, par, i):
                nxt = 1 - par
                if has(k - 1, 0, S):
                    ge(pe, s["x4_ok"], k)
                    ge(pe, s["x4T_ok"], k - 1)
                    transposes(pT4, x4).then_inc(s["x4_tr"], 1)
                if has(k, -1, S - 1):
                    ge(pe, s["x3_ok"], k + 2)
                    ge(pe, s["x3T_ok"], k + 1)
                    transposes(pT3, x3[:, nxt]).then_inc(s["x3_tr"], 1)
                if has(k - 1, 0, S):
                    ge(pe, s["x4T_ok"], k)
                    ge(pe, s["yb_ok"], k - 1)
                    for r in range(R):
                        for c in range(KD):
                            last = mm(pY[:, r * D:(r + 1) * D], x4T[:, c, r * P:(r + 1) * P], wc[:, c, :],
                                      start=c == 0, stop=c == KD - 1)
                    last.then_inc(s["y_mm"], 1)
                if has(k, 0, S):
                    ge(pe, s["p_ok"], k + 1)
                    ge(pe, s["pT_ok"], k)
                    transposes(pPT, pr).then_inc(s["p_tr"], 1)
                if has(k, -1, S - 1):
                    ge(pe, s["diag_ok"], k + 2)
                    ge(pe, s["fac_ok"], k + 1)
                    last = mm(pRow[:, 0:N], ones[:], diag[:, :, :].rearrange("p r n -> p (r n)"), start=True, stop=True)
                    last.then_inc(s["row_mm"], 1)
                    ge(pe, s["x3T_ok"], k + 2)
                    ge(pe, s["sim_ok"], k + 1)
                    for r in range(R):
                        for c in range(KD):
                            last = mm(pDot[:, r * N:(r + 1) * N], x3T[:, c, r * P:(r + 1) * P], x3T[:, c, :],
                                      start=c == 0, stop=c == KD - 1)
                    last.then_inc(s["dot_mm"], 1)
                if has(k, 0, S):
                    ge(pe, s["pT_ok"], k + 1)
                    ge(pe, s["av_ok"], k)
                    for r in range(R):
                        for c in range(R):
                            last = mm(pAV[:, r * D:(r + 1) * D], pT[:, c, r * P:(r + 1) * P], x3[:, par, c, :],
                                      start=c == 0, stop=c == R - 1)
                    last.then_inc(s["av_mm"], 1)
            run(pe, step)

        @block.scalar
        def _(act):
            def step(k, par, i):
                if has(k - 1, 0, S):
                    ge(act, s["x4_tr"], k)
                    ge(act, s["y_mm"], k - 1)
                    nc.scalar.activation(x4T[:], pT4, ACT.Copy).then_inc(s["x4T_ok"], 1)
                if has(k, -1, S - 1):
                    ge(act, s["x3_tr"], k + 2)
                    ge(act, s["dot_mm"], k + 1)
                    nc.scalar.activation(x3T[:], pT3, ACT.Copy).then_inc(s["x3T_ok"], 1)
                if has(k, 0, S):
                    ge(act, s["p_tr"], k + 1)
                    ge(act, s["av_mm"], k)
                    nc.scalar.activation(pT[:], pPT, ACT.Copy).then_inc(s["pT_ok"], 1)
                if has(k - 1, 0, S):
                    ge(act, s["yb_ok"], k)
                    ge(act, s["ho_ok"], k - 1)
                    nc.scalar.activation(th[:], yb[:], ACT.Tanh).then_inc(s["th_ok"], 1)
                if has(k, -1, S - 1):
                    ge(act, s["nm_ok"], k + 2)
                    ge(act, s["p_tr"], k + 1)
                    ge(act, s["rs_ok"], k + 1)
                    for r in range(R):
                        last = nc.scalar.activation(pr[:, r, :], sim[:, r, :], ACT.Exp, bias=nm[:, r:r + 1],
                                                    accum_out=sm[:, r:r + 1])
                    last.then_inc(s["p_ok"], 1)

            run(act, step)

        @block.gpsimd
        def _(pool):
            pl = nc.gpsimd

            def rsqrt(t, n, ve, r):
                ge(pool, s[f"ve{n}_ok"], t + 1)
                pl.tensor_tensor(r[:], ve[:], mhalf[:], ALU.pow).then_inc(s[f"r{n}_ok"], 1)

            def step(k, par, i):
                if has(k, -1, S - 1):
                    rsqrt(k + 1, 3, ve3, r3)
                    ge(pool, s["ssc_ok"], k + 2)
                    ge(pool, s["fac_ok"], k + 1)
                    pl.tensor_tensor(rin[:], ssc[:], mhalf[:], ALU.pow).then_inc(s["rin_ok"], 1)
                if has(k, 0, S):
                    rsqrt(k, 4, ve4, r4)

            run(pool, step)

        @block.vector
        def _(dve):
            v = nc.vector

            def stats(t, n, src, st, mv, ve):
                for r in range(R):
                    last = v.bn_stats(st[:, r, :], src[:, r, :])
                last.then_inc(s[f"st{n}_ok"], 1)
                ge(dve, s[f"st{n}_ok"], t + 1)
                v.tensor_copy(touch[:], st[:, 0, 0:1])
                for r in range(R):
                    last = v.bn_aggr(mv[:, r, :], st[:, r, :])
                last.then_inc(s[f"mv{n}_ok"], 1)
                ge(dve, s[f"mv{n}_ok"], t + 1)
                ge(dve, s[f"r{n}_ok"], t)
                v.tensor_scalar(ve[:], mv[:, :, 1], EPS, None, ALU.add).then_inc(s[f"ve{n}_ok"], 1)

            def normed(t, n, dst, src, mv, rr):
                ge(dve, s[f"r{n}_ok"], t + 1)
                for r in range(R):
                    last = v.tensor_scalar(dst[:, r, :], src[:, r, :], mv[:, r, 0:1], rr[:, r:r + 1],
                                           ALU.subtract, ALU.mult)
                last.then_inc(s[f"x{n}_ok"], 1)

            def step(k, par, i):
                nxt = 1 - par
                if has(k, -1, S - 1):
                    if par:
                        ge(dve, h_in[0], 16 * (i + 2))
                    else:
                        ge(dve, h_in[1], 16 * (i + 1))
                    stats(k + 1, 3, hin[:, nxt], st3, mv3, ve3)
                    ge(dve, s["av_ok"], k)
                    normed(k + 1, 3, x3[:, nxt], hin[:, nxt], mv3, r3)
                    ge(dve, s["x3_ok"], k + 2)
                    v.tensor_tensor(sq[:], x3[:, nxt], x3[:, nxt], ALU.mult).then_inc(s["sq_ok"], 1)
                    ge(dve, s["sq_ok"], k + 2)
                    v.tensor_reduce(ss[:], sq[:], AX.X, ALU.add).then_inc(s["ss_ok"], 1)
                    ge(dve, s["ss_ok"], k + 2)
                    v.tensor_scalar(ssc[:], ss[:], 1e-36, None, ALU.max).then_inc(s["ssc_ok"], 1)
                    ge(dve, s["rin_ok"], k + 2)
                    ge(dve, s["row_mm"], k + 1)
                    for r in range(R):
                        last = v.tensor_scalar(diag[:, r, :], ident[:], rin[:, r:r + 1], None, ALU.mult)
                    last.then_inc(s["diag_ok"], 1)
                if has(k - 1, 0, S):
                    ge(dve, s["y_mm"], k)
                    ge(dve, s["th_ok"], k - 1)
                    v.tensor_tensor(yb[:], pY.rearrange("p (r d) -> p r d", r=R),
                                    bias[:, :].unsqueeze(1).broadcast_to([P, R, D]), ALU.add).then_inc(s["yb_ok"], 1)
                if has(k, -1, S - 1):
                    ge(dve, s["row_mm"], k + 2)
                    for r in range(R):
                        last = v.tensor_scalar(fac[:, r, :], pRow[:, 0:N], rin[:, r:r + 1], 1e8, ALU.mult, ALU.min)
                    last.then_inc(s["fac_ok"], 1)
                    ge(dve, s["dot_mm"], k + 2)
                    ge(dve, s["fac_ok"], k + 2)
                    ge(dve, s["p_ok"], k + 1)
                    v.tensor_tensor(sim[:], pDot.rearrange("p (r n) -> p r n", r=R), fac[:], ALU.mult)\
                        .then_inc(s["sim_ok"], 1)
                    ge(dve, s["sim_ok"], k + 2)
                    v.tensor_reduce(nm[:], sim[:], AX.X, ALU.max, negate=True).then_inc(s["nm_ok"], 1)
                if has(k - 1, 0, S):
                    ge(dve, s["th_ok"], k)
                    ge(dve, o_out[1 - par], 16 * (i - (0 if par else 1)))
                    v.tensor_tensor(ho[:, 1 - par], th[:], h4[:, 1 - par], ALU.add).then_inc(s["ho_ok"], 1)
                if has(k, 0, S):
                    ge(dve, s["av_mm"], k + 1)
                    for r in range(R):
                        last = v.scalar_tensor_tensor(av[:, r, :], pAV[:, r * D:(r + 1) * D], rs[:, par, r:r + 1],
                                                      x3[:, par, r, :], ALU.mult, ALU.add)
                    last.then_inc(s["av_ok"], 1)
                    ge(dve, s["av_ok"], k + 1)
                    v.tensor_tensor(h4[:, par], av[:], hin[:, par], ALU.add).then_inc(s["h4_ok"], 1)
                    ge(dve, s["h4_ok"], k + 1)
                    stats(k, 4, h4[:, par], st4, mv4, ve4)
                    ge(dve, s["x4_tr"], k)
                    normed(k, 4, x4, h4[:, par], mv4, r4)
                if has(k, -1, S - 1):
                    ge(dve, s["p_ok"], k + 2)
                    v.reciprocal(rs[:, nxt, :], sm[:]).then_inc(s["rs_ok"], 1)

            run(dve, step)


def build(nc, io):
    ctx = ExitStack()
    with ctx:
        def sb(name, shape, dt=F32):
            return ctx.enter_context(nc.sbuf_tensor(name, shape, dt))

        keep = {
            "ident": sb("ident", [P, P]), "mask": sb("mask", [P, P]),
            "h2": sb("h2_all", [P, NT, D]), "lg": sb("lg_all", [P, NT, E]),
            "slots": sb("slots", [P, 2, NT], I32), "prob": sb("prob", [P, 2, NT]),
            "tile_expert": sb("tile_expert", [P, NS], I32),
            "ps": ctx.enter_context(nc.psum_tensor("ps", [P, 4096], F32)),
            "xs": nc.dram_tensor("xs", (NS * P, D), F32, kind="Internal").ap(),
            "ys": nc.dram_tensor("ys", (NS * P, D), F32, kind="Internal").ap(),
            "hb": nc.dram_tensor("hb", (S, N, D), F32, kind="Internal").ap(),
        }
        for n in ("xs_zero", "ws_in", "w_in"):
            keep[n] = ctx.enter_context(nc.semaphore(n))
        with ExitStack() as first:
            for n, shape in (("x2", [P, NT, D]), ("x2T", [P, NT, KD, P]), ("ws12", [P, 2, KD, 2 * HE]),
                             ("ws3", [P, 2, KH, D]), ("zeros", [P, D])):
                keep[n] = first.enter_context(nc.sbuf_tensor(n + "_all", shape, F32))
            with ExitStack() as stage:
                attention_stage(nc, stage, io, keep)
            for n, shape in (("w12", [P, E, KD, 2 * HE]), ("w3", [P, E, KH, D])):
                keep[n] = first.enter_context(nc.sbuf_tensor(n + "_all", shape, F32))
            with nc.Block() as block:
                @block.sync
                def _(sp):
                    sp.dma_start(keep["w12"][:], io["w12"]).then_inc(keep["w_in"], 16)
                    sp.dma_start(keep["w3"][:], io["w3"]).then_inc(keep["w_in"], 16)
            with ExitStack() as stage:
                shared_stage(nc, stage, io, keep)
            with ExitStack() as stage:
                routed_stage(nc, stage, io, keep)
        with ExitStack() as stage:
            final_stage(nc, stage, io, keep)


def layout(inputs):
    a = {k: np.asarray(v) for k, v in inputs.items()}
    x = a["x"].reshape(S, 5, 16, 8, 16, 8)
    x = x.transpose(1, 3, 5, 2, 4, 0).reshape(FEAT, T)
    xp = np.zeros((KF * P, T), x.dtype)
    xp[:FEAT] = x
    xp = xp.reshape(KF, P, NT, P).transpose(2, 1, 0, 3)
    wt = np.zeros((KF * P, D), x.dtype)
    wt[:FEAT] = a["L0_tok_W"]

    def rows(m):
        return m.reshape(-1, P, m.shape[1]).transpose(1, 0, 2)

    qc = np.zeros((HP, P, P), x.dtype)
    q_c = a["L0_attn_q_c"].reshape(C, H, DH)
    for h in range(H):
        j, e = h // 2, h % 2
        qc[j, 32 * (j % 4) + DH * e:32 * (j % 4) + DH * (e + 1), C * e:C * (e + 1)] = q_c[:, h, :].T
    small = np.zeros((P, 8), x.dtype)
    small[:, 0:2] = a["L0_attn_bq"].reshape(KD, P).T
    small[:, 2:4] = a["L0_attn_bk"].reshape(KD, P).T
    small[:, 4:6] = np.repeat(a["L0_attn_beta"], DH).reshape(KD, P).T
    head = np.arange(P) // DH
    small[:, 6] = head % 2 == 0
    small[:, 7] = head % 2 == 1
    n, s = np.arange(P) // S, np.arange(P) % S
    mask = ((n[:, None] == n[None, :]) & (s[:, None] <= s[None, :])).astype(x.dtype)
    def chunks(m, k):
        full = np.zeros(m.shape[:-2] + (k * P, m.shape[-1]), m.dtype)
        full[..., :m.shape[-2], :] = m
        full = full.reshape(m.shape[:-2] + (k, P, m.shape[-1]))
        return np.moveaxis(full, -2, 0)

    w12 = np.concatenate([a["L0_ffn_W1"], a["L0_ffn_W2"]], -1)
    ws12 = np.stack([np.concatenate([a["L0_ffn_Ws1"][:, n * HE:(n + 1) * HE], a["L0_ffn_Ws2"][:, n * HE:(n + 1) * HE]], -1)
                     for n in range(2)])
    ws3 = a["L0_ffn_Ws3"].reshape(2, HE, D)
    rc = np.zeros((P, RC), x.dtype)
    rc[:, 0:NT] = np.arange(NT) * P
    rc[:, NT:NT + E] = E - np.arange(E)
    rc[:, NT + E:] = np.arange(NS)
    idx = np.arange(P)
    out = {
        "w12": chunks(w12, KD), "w3": chunks(a["L0_ffn_W3"], KH), "ws12": chunks(ws12, KD), "ws3": chunks(ws3, KH),
        "rc": rc, "strict": (idx[:, None] < idx[None, :]).astype(x.dtype), "ones": np.ones((P, P), x.dtype),
        "l1w": rows(a["L1_ffn_weight"].T), "l1a1": rows(a["L1_ffn_aux_weight1"]), "l1a2": rows(a["L1_ffn_aux_weight2"]),
        "l1b": a["L1_ffn_bias"],
        "x": xp, "wtok": rows(wt), "gamma": a["L0_tok_gamma"], "small": small, "qc": qc.transpose(1, 0, 2),
        "wq": rows(a["L0_attn_Wq"].T), "wk": rows(a["L0_attn_Wk"].T), "wv": rows(a["L0_attn_Wv"].T),
        "wo": rows(a["L0_attn_Wo"].T), "bv": a["L0_attn_bv"], "bo": a["L0_attn_bo"], "wg": rows(a["L0_ffn_Wg"]),
        "ident": np.eye(P, dtype=x.dtype), "mask": mask,
    }
    return {k: np.ascontiguousarray(v) for k, v in out.items()}


OUTS = {"out": (S, N, D)}


def kernel(**inputs):
    import concourse.bacc as bacc
    from concourse.bass_utils import run_bass_kernel_spmd

    arrays = layout(inputs)
    nc = bacc.Bacc("TRN2", target_bir_lowering=False, num_devices=1)
    io = {n: nc.dram_tensor("in_" + n, a.shape, mybir.dt.from_np(a.dtype), kind="ExternalInput").ap()
          for n, a in arrays.items()}
    for n, shape in OUTS.items():
        io[n] = nc.dram_tensor(n, shape, F32, kind="ExternalOutput").ap()
    build(nc, io)
    r = run_bass_kernel_spmd(nc, [{"in_" + n: a for n, a in arrays.items()}], core_ids=[0])
    return r.results[0]["out"]
```

```python
import numpy as np
import concourse.bass as bass
from concourse import mybir
from contextlib import ExitStack

F32 = mybir.dt.float32
F16 = mybir.dt.float16
I32 = mybir.dt.int32
U32 = mybir.dt.uint32
ALU = mybir.AluOpType
ACT = mybir.ActivationFunctionType
AX = mybir.AxisListType

P = 128
S = 8
N = 256
T = S * N
NT = T // P
D = 256
KD = D // P
FEAT = 320
KF = 3
FK = [P, P, FEAT - 2 * P]
H = 16
DH = D // H
C = 64
HP = H // 2
VW = DH + 1
E = 8
HE = 352
KH = 3
HK = [P, P, HE - 2 * P]
TOP = 2
NS = (TOP * T + E * (P - 1)) // P
RC = NT + E + NS
ONEHOT, DIFF = 13, 14
EPS = 1e-5


def ge(eng, sem, value):
    if isinstance(value, int) and value <= 0:
        return
    eng.wait_ge(sem, value)


def bc(ap, shape):
    return ap.unsqueeze(2).broadcast_to(shape)


def steps(eng, body):
    for k in range(-1, 4):
        body(k, k % 2)
    with eng.Fori(2, NT // 2 - 1) as i:
        body(i * 2, 0)
        body(i * 2 + 1, 1)
    for k in range(NT - 2, NT + 2):
        body(k, k % 2)


def upto(t):
    return min(t, NT) if isinstance(t, int) else t


def has(k, lo, hi):
    return not isinstance(k, int) or lo <= k < hi


def attention_stage(nc, ctx, io, keep):

    def sb(name, shape, dt=F32):
        return ctx.enter_context(nc.sbuf_tensor(name, shape, dt))

    def sem(name):
        return ctx.enter_context(nc.semaphore(name))

    wtok = sb("wtok", [P, KF, D])
    gamma = sb("gamma", [P, D])
    wq = sb("wq", [P, KD, D])
    wk = sb("wk", [P, KD, D])
    wv = sb("wv", [P, KD, D])
    wo = sb("wo", [P, KD, D])
    qc = sb("qc", [P, HP, P])
    small = sb("small", [P, 8])
    bv = sb("bv", [P, D])
    bo = sb("bo", [P, D])
    wg = sb("wg", [P, KD, E])
    ident, mask = keep["ident"], keep["mask"]
    h2_all, x2_all, x2T_all, lg_all = keep["h2"], keep["x2"], keep["x2T"], keep["lg"]

    qscale = sb("qscale", [P, KD, 2])
    expb = sb("expb", [P, KD])
    mhalf, touch = sb("mhalf", [P, 1]), sb("touch", [P, 1])
    xt = sb("xt", [P, 2, KF, P])
    st0, mv0, ve0, r0 = sb("st0", [P, 6]), sb("mv0", [P, 2]), sb("ve0", [P, 1]), sb("r0", [P, 1])
    st1, mv1, ve1, r1 = sb("st1", [P, 6]), sb("mv1", [P, 2]), sb("ve1", [P, 1]), sb("r1", [P, 1])
    st2, mv2, ve2, r2 = sb("st2", [P, 6]), sb("mv2", [P, 2]), sb("ve2", [P, 1]), sb("r2", [P, 1])
    h0 = sb("h0", [P, D])
    x1 = sb("x1", [P, D])
    x1T = sb("x1T", [P, KD, P])
    qz = sb("qz", [P, KD, 2, P])
    kT = sb("kT", [P, KD, P])
    vf = sb("vf", [P, H, DH])
    v1 = sb("v1", [P, 2, 2, H, VW], F16)
    mx = sb("mx", [P, P])
    cwd = sb("cwd", [P, HP, P])
    cwT = sb("cwT", [P, 2, HP, P])
    cw = sb("cw", [P, HP * P])
    qkm = sb("qkm", [P, 2, HP, P])
    ln = sb("ln", [P, H * C])
    rn = sb("rn", [P, H * C])
    sc = sb("sc", [P, H, C])
    scm = sb("scm", [P, H])
    scd = sb("scd", [P, H, C])
    ex = sb("ex", [P, H * C])
    w = sb("w", [P, HP, P])
    wT = sb("wT", [P, HP, P])
    am = sb("am", [P, 2, HP, P])
    amh, aml = sb("amh", [P, 2, HP, P], F16), sb("aml", [P, 2, HP, P], F16)
    rz = sb("rz", [P, H])
    on = sb("on", [P, H, DH])
    oT = sb("oT", [P, KD, P])
    yb = sb("yb", [P, D])
    x2 = sb("x2", [P, D])
    x2T = sb("x2T", [P, KD, P])

    ps = keep["ps"]
    S0, S1 = ps[:, 0:512], ps[:, 512:1024]
    X, Y, Z = ps[:, 1024:2048], ps[:, 2048:3072], ps[:, 3072:4096]
    pTok, pV = S0[:, 0:D], S0[:, 0:D]
    pQK, pO = S1, S1[:, 0:H * VW]
    pY, pLg = X[:, 0:D], X[:, 512:512 + E]
    pX1T, pX2T, pOT = Z[:, 0:D], Z[:, 512:512 + D], Z[:, 512:512 + D]

    names = """tok_mm x1_tr qk_mm v_mm cwT_mm qka_mm qkb_mm cw_tr norm_mm s_mm w_tr aa_mm ab_mm o_mm o_tr
        y_mm x2_tr lg_mm  x1T_ok kT_ok ln_ok rn_ok e_ok cwT_ok cw_ok wT_ok oT_ok x2T_ok
        st0_ok mv0_ok st1_ok mv1_ok st2_ok mv2_ok ve0_ok r0_ok ve1_ok r1_ok ve2_ok r2_ok h0_ok h1_ok
        x1_ok qz_ok v_ok mx_ok cwd_ok qkma_ok qkmb_ok sc_ok scm_ok scd_ok ama_ok amb_ok amha_ok amhb_ok amla_ok amlb_ok vf_ok vh_ok rz_ok on_ok
        yb_ok h2_ok x2_ok lg_ok w_ok x2c_ok x2Tc_ok""".split()
    s = {n: sem("A_" + n) for n in names}
    x_in = [sem("A_x_in0"), sem("A_x_in1")]
    w_in = sem("A_w_in")
    c_ok = sem("A_c_ok")
    z_ok = sem("A_z_ok")

    loads = [(wtok, io["wtok"]), (gamma, io["gamma"].partition_broadcast(P)), (wq, io["wq"]), (wk, io["wk"]),
             (wv, io["wv"]), (small, io["small"]), (bv, io["bv"].partition_broadcast(P)), (ident, io["ident"]),
             (mask, io["mask"]), (qc, io["qc"]), (wo, io["wo"]), (bo, io["bo"].partition_broadcast(P)),
             (wg, io["wg"])]
    ALL_IN = 16 * len(loads)

    with nc.Block() as block:

        @block.sync
        def _(sp):
            sp.dma_start(xt[:, 0], io["x"][0]).then_inc(x_in[0], 16)
            for dst, src in loads[:2]:
                sp.dma_start(dst[:], src).then_inc(w_in, 16)
            sp.dma_start(xt[:, 1], io["x"][1]).then_inc(x_in[1], 16)
            for dst, src in loads[2:]:
                sp.dma_start(dst[:], src).then_inc(w_in, 16)

            def load(t, par):
                ge(sp, s["tok_mm"], t - 1)
                sp.dma_start(xt[:, par], io["x"][t]).then_inc(x_in[par], 16)

            sp.dma_start(keep["ws12"][:], io["ws12"]).then_inc(keep["ws_in"], 16)
            sp.dma_start(keep["ws3"][:], io["ws3"]).then_inc(keep["ws_in"], 16)
            sp.wait_ge(z_ok, 1)
            sp.dma_start(keep["xs"].rearrange("(p j) d -> p j d", p=P),
                         keep["zeros"][:, :].unsqueeze(1).broadcast_to([P, NS, D])).then_inc(keep["xs_zero"], 16)
            with sp.Fori(1, NT // 2) as i:
                load(i * 2, 0)
                load(i * 2 + 1, 1)
            sp.wait_ge(keep["ws_in"], 32)

        @block.tensor
        def _(pe):
            mm, tr = nc.tensor.matmul, nc.tensor.transpose

            def tok(t, par, half):
                ge(pe, x_in[par], (half + 1) * 16)
                ge(pe, s["vf_ok"], t)
                for c in range(KF):
                    last = mm(pTok, xt[0:FK[c], par, c, :], wtok[0:FK[c], c, :], start=c == 0, stop=c == KF - 1)
                last.then_inc(s["tok_mm"], 1)

            def norms(t):
                ge(pe, s["cw_ok"], t + 1)
                ge(pe, s["ama_ok"], t)
                for c in range(2):
                    last = mm(X[:, c * 512:(c + 1) * 512], mask[:], cw[:, c * 512:(c + 1) * 512], start=True, stop=True)
                last.then_inc(s["norm_mm"], 1)

            def x2_transpose(t):
                ge(pe, s["x2_ok"], t + 1)
                ge(pe, s["cw_ok"], upto(t + 3))
                for c in range(KD):
                    last = tr(pX2T[:, c * P:(c + 1) * P], x2[:, c * P:(c + 1) * P], ident[:])
                last.then_inc(s["x2_tr"], 1)

            def scores(t):
                ge(pe, s["qkma_ok"], t + 1)
                ge(pe, s["qkmb_ok"], t + 1)
                ge(pe, s["amb_ok"], t)
                for h in range(H):
                    j, e = h // 2, h % 2
                    last = mm(Y[:, h * C:(h + 1) * C], qkm[:, (j % 4) // 2, (j % 2) * 4 + (j // 4) * 2 + e, :],
                              cw[:, h * C:(h + 1) * C], start=True, stop=True)
                last.then_inc(s["s_mm"], 1)

            def x1_transpose(t):
                ge(pe, s["x1_ok"], t + 1)
                ge(pe, s["cw_ok"], t)
                for c in range(KD):
                    last = tr(pX1T[:, c * P:(c + 1) * P], x1[:, c * P:(c + 1) * P], ident[:])
                last.then_inc(s["x1_tr"], 1)

            def values(t, par):
                ge(pe, s["amhb_ok"], t + 1)
                ge(pe, s["amla_ok"], t + 1)
                ge(pe, s["amlb_ok"], t + 1)
                ge(pe, s["v_ok"], t + 1)
                ge(pe, s["kT_ok"], upto(t + 2))
                for h in range(H):
                    j, e = h // 2, h % 2
                    for n, (a, b) in enumerate(((amh, 0), (amh, 1), (aml, 0))):
                        last = mm(pO[:, h * VW:(h + 1) * VW], a[:, j // 4, e * 4 + j % 4, :], v1[:, par, b, h, :],
                                  start=n == 0, stop=n == 2)
                last.then_inc(s["o_mm"], 1)

            def router(t):
                ge(pe, s["x2T_ok"], t + 1)
                ge(pe, s["ln_ok"], upto(t + 3))
                for c in range(KD):
                    last = mm(pLg, x2T[:, c, :], wg[:, c, :], start=c == 0, stop=c == KD - 1)
                last.then_inc(s["lg_mm"], 1)

            def project_qk(t):
                ge(pe, s["x1T_ok"], t + 1)
                ge(pe, s["on_ok"], t - 1)
                for n, wt in enumerate((wq, wk)):
                    for m in range(KD):
                        for c in range(KD):
                            last = mm(pQK[:, (2 * n + m) * P:(2 * n + m + 1) * P], wt[:, c, m * P:(m + 1) * P],
                                      x1T[:, c, :], start=c == 0, stop=c == KD - 1)
                last.then_inc(s["qk_mm"], 1)

            def o_transpose(t):
                ge(pe, s["on_ok"], t + 1)
                ge(pe, s["x2T_ok"], t)
                for c in range(KD):
                    last = tr(pOT[:, c * P:(c + 1) * P], on[:, :, :].rearrange("p h d -> p (h d)")[:, c * P:(c + 1) * P],
                              ident[:])
                last.then_inc(s["o_tr"], 1)

            def project_v(t):
                ge(pe, s["h0_ok"], t + 1)
                for c in range(KD):
                    last = mm(pV, x1T[:, c, :], wv[:, c, :], start=c == 0, stop=c == KD - 1)
                last.then_inc(s["v_mm"], 1)

            def out_project(t):
                ge(pe, s["oT_ok"], t + 1)
                ge(pe, s["ln_ok"], upto(t + 2))
                for c in range(KD):
                    last = mm(pY, oT[:, c, :], wo[:, c, :], start=c == 0, stop=c == KD - 1)
                last.then_inc(s["y_mm"], 1)

            def w_transpose(t):
                ge(pe, s["w_ok"], t + 1)
                ge(pe, s["x1T_ok"], upto(t + 2))
                ge(pe, s["oT_ok"], t)
                for j in range(HP):
                    last = tr(Z[:, j * P:(j + 1) * P], w[:, j, :], ident[:])
                last.then_inc(s["w_tr"], 1)

            def qk(t, half):
                ge(pe, s["qz_ok"], t + 1)
                ge(pe, s["kT_ok"], t + 1)
                out = Y if half else X
                if half:
                    ge(pe, s["sc_ok"], t)
                else:
                    ge(pe, s["yb_ok"], t - 1)
                    ge(pe, s["lg_ok"], t - 2)
                for j in (0, 1, 4, 5):
                    j += 2 * half
                    at = (j % 2) * 512 + (j // 4) * D
                    rows = slice(32 * (j % 4), 32 * (j % 4) + 32)
                    last = mm(out[:, at:at + D].rearrange("p (e n) -> p e n", e=2), kT[rows, j // 4, :],
                              qz[rows, j // 4, :, :], start=True, stop=True)
                last.then_inc(s["qkb_mm" if half else "qka_mm"], 1)

            def cw_logits(t):
                ge(pe, s["wT_ok"], t)
                for j in range(HP):
                    last = mm(Z[:, j * P:(j + 1) * P], qc[:, j, :], kT[:, j // 4, :], start=True, stop=True)
                last.then_inc(s["cwT_mm"], 1)

            def weights_of_values(t, par):
                ge(pe, s["wT_ok"], t + 1)
                ge(pe, s["cwT_ok"], t + 1)
                ge(pe, s["yb_ok"], t)
                ge(pe, s["lg_ok"], t - 1)
                ge(pe, s["sc_ok"], t + 1)
                for half, out in enumerate((X, Y)):
                    ge(pe, s["qkmb_ok" if half else "qkma_ok"], upto(t + 2))
                    for jj in range(4):
                        for e in range(2):
                            at = e * 512 + jj * P
                            rows = slice(64 * e, 64 * e + 64)
                            last = mm(out[:, at:at + P], cwT[rows, par, 4 * half + jj, :],
                                      wT[rows, 4 * half + jj, :], start=True, stop=True)
                    last.then_inc(s["ab_mm" if half else "aa_mm"], 1)

            def cw_transpose(t, par):
                ge(pe, s["cwT_ok"], t + 1)
                ge(pe, s["cwd_ok"], t + 1)
                for j in range(HP):
                    last = tr(Z[:, j * P:(j + 1) * P], cwT[:, par, j, :], ident[:])
                last.then_inc(s["cw_tr"], 1)

            def step(k, par, half):
                front, mid, back, end = has(k, -1, NT - 1), has(k, 0, NT), has(k - 1, 0, NT), has(k - 2, 0, NT)
                if front:
                    tok(k + 1, 1 - par, half)
                if mid:
                    norms(k)
                if end:
                    x2_transpose(k - 2)
                if mid:
                    scores(k)
                if front:
                    x1_transpose(k + 1)
                if back:
                    values(k - 1, 1 - par)
                if end:
                    router(k - 2)
                if front:
                    project_qk(k + 1)
                if back:
                    o_transpose(k - 1)
                if front:
                    project_v(k + 1)
                if back:
                    out_project(k - 1)
                if front:
                    qk(k + 1, 1)
                if mid:
                    w_transpose(k)
                if front:
                    qk(k + 1, 0)
                    cw_logits(k + 1)
                if mid:
                    weights_of_values(k, par)
                if front:
                    cw_transpose(k + 1, 1 - par)

            pe.wait_ge(w_in, ALL_IN)
            for k in range(-1, 4):
                step(k, k % 2, (k + 1) // 2)
            with pe.Fori(2, NT // 2 - 1) as i:
                step(i * 2, 0, i)
                step(i * 2 + 1, 1, i + 1)
            for k in range(NT - 2, NT + 2):
                step(k, k % 2, (k + 1) // 2)

        @block.scalar
        def _(act):
            act.wait_ge(w_in, ALL_IN)
            nc.scalar.preload_act_table_set("natural_log_exp_and_others")
            nc.scalar.activation(expb[:], small[:, 4:6], ACT.Exp, scale=-1.0).then_inc(c_ok, 1)

            def step(k, par):
                nxt = 1 - par
                if has(k, 0, NT):
                    ge(act, s["norm_mm"], k + 1)
                    nc.scalar.activation(ln[:], X, ACT.Ln).then_inc(s["ln_ok"], 1)
                    ge(act, s["ln_ok"], k + 1)
                    ge(act, s["w_ok"], k)
                    nc.scalar.activation(rn[:], ln[:], ACT.Exp, scale=-1.0).then_inc(s["rn_ok"], 1)
                if has(k - 2, 0, NT):
                    ge(act, s["x2_tr"], k - 1)
                    ge(act, s["x2Tc_ok"], k - 2)
                    ge(act, s["lg_mm"], k - 2)
                    nc.scalar.activation(x2T[:], pX2T, ACT.Copy).then_inc(s["x2T_ok"], 1)
                if has(k, -1, NT - 1):
                    ge(act, s["x1_tr"], k + 2)
                    ge(act, s["v_mm"], k + 1)
                    nc.scalar.activation(x1T[:], pX1T, ACT.Copy).then_inc(s["x1T_ok"], 1)
                if has(k, 0, NT):
                    ge(act, s["scd_ok"], k + 1)
                    ge(act, s["w_ok"], k)
                    nc.scalar.activation(ex[:], scd[:, :, :].rearrange("p h c -> p (h c)"), ACT.Exp)\
                        .then_inc(s["e_ok"], 1)
                if has(k - 1, 0, NT):
                    ge(act, s["o_tr"], k)
                    ge(act, s["y_mm"], k - 1)
                    nc.scalar.activation(oT[:], pOT, ACT.Copy).then_inc(s["oT_ok"], 1)
                if has(k, 0, NT):
                    ge(act, s["w_tr"], k + 1)
                    ge(act, s["ab_mm"], k)
                    nc.scalar.activation(wT[:], Z, ACT.Copy).then_inc(s["wT_ok"], 1)
                if has(k, -1, NT - 1):
                    ge(act, s["cwd_ok"], k + 2)
                    ge(act, s["ab_mm"], k)
                    nc.scalar.activation(cwT[:, nxt], cwd[:], ACT.Exp).then_inc(s["cwT_ok"], 1)
                if has(k, 0, NT):
                    ge(act, s["ama_ok"], k + 1)
                    ge(act, s["o_mm"], k)
                    nc.scalar.activation(amh[:, 0], am[:, 0], ACT.Copy).then_inc(s["amha_ok"], 1)
                if has(k, -1, NT - 1):
                    ge(act, s["cw_tr"], k + 2)
                    ge(act, s["s_mm"], k + 1)
                    nc.scalar.activation(cw[:], Z, ACT.Copy).then_inc(s["cw_ok"], 1)
                if has(k, 0, NT):
                    ge(act, s["amb_ok"], k + 1)
                    nc.scalar.activation(amh[:, 1], am[:, 1], ACT.Copy).then_inc(s["amhb_ok"], 1)

            steps(act, step)

        @block.gpsimd
        def _(pool):
            nc.gpsimd.memset(mhalf[:], -0.5).then_inc(c_ok, 1)
            nc.gpsimd.memset(keep["zeros"][:], 0.0).then_inc(z_ok, 1)
            pool.wait_ge(c_ok, 2)

            def rsqrt(t, n, ve, r):
                ge(pool, s[f"ve{n}_ok"], t + 1)
                nc.gpsimd.tensor_tensor(r[:], ve[:], mhalf[:], ALU.pow).then_inc(s[f"r{n}_ok"], 1)

            def low(t, n):
                ge(pool, s["amhb_ok" if n else "amha_ok"], t + 1)
                ge(pool, s["o_mm"], t)
                nc.gpsimd.tensor_tensor(aml[:, n], am[:, n], amh[:, n], ALU.subtract)\
                    .then_inc(s["amlb_ok" if n else "amla_ok"], 1)

            def step(k, par):
                if has(k - 1, 0, NT):
                    low(k - 1, 0)
                if has(k, -1, NT - 1):
                    rsqrt(k + 1, 0, ve0, r0)
                if has(k - 1, 0, NT):
                    low(k - 1, 1)
                if has(k, -1, NT - 1):
                    rsqrt(k + 1, 1, ve1, r1)
                if has(k - 2, 0, NT):
                    ge(pool, s["x2_ok"], k - 1)
                    nc.gpsimd.tensor_copy(x2_all[:, k - 2, :], x2[:]).then_inc(s["x2c_ok"], 1)
                    ge(pool, s["x2T_ok"], k - 1)
                    nc.gpsimd.tensor_copy(x2T_all[:, k - 2, :, :], x2T[:]).then_inc(s["x2Tc_ok"], 1)
                if has(k, 0, NT):
                    ge(pool, s["e_ok"], k + 1)
                    ge(pool, s["w_tr"], k)
                    nc.gpsimd.tensor_tensor(w[:, :, :].rearrange("p j c -> p (j c)"), ex[:], rn[:], ALU.mult)\
                        .then_inc(s["w_ok"], 1)
                if has(k - 1, 0, NT):
                    rsqrt(k - 1, 2, ve2, r2)

            steps(pool, step)

        @block.vector
        def _(dve):
            dve.wait_ge(w_in, ALL_IN)
            for n in range(2):
                nc.vector.memset(v1[:, :, n, :, DH:VW], 1.0 - n).then_inc(c_ok, 1)
            dve.wait_ge(c_ok, 4)
            for c in range(KD):
                for e in range(2):
                    last = nc.vector.tensor_scalar(qscale[:, c, e:e + 1], small[:, 6 + e:7 + e], expb[:, c:c + 1],
                                                   DH ** -0.5, ALU.mult, ALU.mult)
            last.then_inc(c_ok, 1)
            dve.wait_ge(c_ok, 5)

            def stats(t, n, src, st, mv, ve):
                nc.vector.bn_stats(st[:], src).then_inc(s[f"st{n}_ok"], 1)
                ge(dve, s[f"st{n}_ok"], t + 1)
                nc.vector.tensor_copy(touch[:], st[:, 0:1])
                nc.vector.bn_aggr(mv[:], st[:]).then_inc(s[f"mv{n}_ok"], 1)
                ge(dve, s[f"mv{n}_ok"], t + 1)
                ge(dve, s[f"r{n}_ok"], t)
                nc.vector.tensor_scalar(ve[:], mv[:, 1:2], EPS, None, ALU.add).then_inc(s[f"ve{n}_ok"], 1)

            def masked(src, dst, done):
                nc.vector.tensor_tensor(dst, src.rearrange("p (j n) -> p j n", j=HP),
                                        mask[:, :].unsqueeze(1).broadcast_to([P, HP, P]), ALU.mult).then_inc(s[done], 1)

            def step(k, par):
                nxt = 1 - par
                front, mid, back, end = has(k, -1, NT - 1), has(k, 0, NT), has(k - 1, 0, NT), has(k - 2, 0, NT)
                if front:
                    ge(dve, s["tok_mm"], k + 2)
                    stats(k + 1, 0, pTok, st0, mv0, ve0)
                    ge(dve, s["r0_ok"], k + 2)
                    nc.vector.tensor_scalar(h0[:], pTok, mv0[:, 0:1], r0[:], ALU.subtract, ALU.mult)\
                        .then_inc(s["h0_ok"], 1)
                    ge(dve, s["h0_ok"], k + 2)
                    nc.vector.tensor_tensor(h2_all[:, k + 1, :], h0[:], gamma[:], ALU.mult).then_inc(s["h1_ok"], 1)
                    ge(dve, s["h1_ok"], k + 2)
                    nc.vector.tensor_copy(touch[:], mv0[:, 0:1])
                    stats(k + 1, 1, h2_all[:, k + 1, :], st1, mv1, ve1)
                    ge(dve, s["r1_ok"], k + 2)
                    ge(dve, s["x1_tr"], k + 1)
                    nc.vector.tensor_scalar(x1[:], h2_all[:, k + 1, :], mv1[:, 0:1], r1[:], ALU.subtract, ALU.mult)\
                        .then_inc(s["x1_ok"], 1)
                if mid:
                    ge(dve, s["s_mm"], k + 1)
                    ge(dve, s["rn_ok"], k + 1)
                    nc.vector.tensor_tensor(sc[:, :, :].rearrange("p h c -> p (h c)"), Y, rn[:], ALU.mult)\
                        .then_inc(s["sc_ok"], 1)
                if back:
                    ge(dve, s["o_mm"], k)
                    pOh = pO.rearrange("p (h d) -> p h d", h=H)
                    nc.vector.reciprocal(rz[:], pOh[:, :, DH]).then_inc(s["rz_ok"], 1)
                    ge(dve, s["rz_ok"], k)
                    ge(dve, s["o_tr"], k - 1)
                    nc.vector.tensor_tensor(on[:], pOh[:, :, 0:DH], bc(rz[:, :], [P, H, DH]), ALU.mult)\
                        .then_inc(s["on_ok"], 1)
                if mid:
                    ge(dve, s["sc_ok"], k + 1)
                    nc.vector.tensor_reduce(scm[:], sc[:], AX.X, ALU.max).then_inc(s["scm_ok"], 1)
                    ge(dve, s["scm_ok"], k + 1)
                    ge(dve, s["e_ok"], k)
                    nc.vector.tensor_tensor(scd[:], sc[:], bc(scm[:, :], [P, H, C]), ALU.subtract)\
                        .then_inc(s["scd_ok"], 1)
                if end:
                    ge(dve, s["lg_mm"], k - 1)
                    nc.vector.tensor_copy(lg_all[:, k - 2, :], pLg).then_inc(s["lg_ok"], 1)
                if front:
                    ge(dve, s["qk_mm"], k + 2)
                    ge(dve, s["qka_mm"], k + 1)
                    ge(dve, s["cwT_mm"], k + 1)
                    for c in range(KD):
                        for e in range(2):
                            last = nc.vector.tensor_scalar(qz[:, c, e, :], pQK[:, c * P:(c + 1) * P], small[:, c:c + 1],
                                                           qscale[:, c, e:e + 1], ALU.add, ALU.mult)
                    last.then_inc(s["qz_ok"], 1)
                    for c in range(KD):
                        last = nc.vector.tensor_scalar(kT[:, c, :], pQK[:, (2 + c) * P:(3 + c) * P],
                                                       small[:, 2 + c:3 + c], None, ALU.add)
                    last.then_inc(s["kT_ok"], 1)
                    ge(dve, s["v_mm"], k + 2)
                    ge(dve, s["o_mm"], k)
                    nc.vector.tensor_tensor(vf[:], pV.rearrange("p (h d) -> p h d", h=H),
                                            bv[:, :].rearrange("p (h d) -> p h d", h=H), ALU.add).then_inc(s["vf_ok"], 1)
                    ge(dve, s["vf_ok"], k + 2)
                    nc.vector.tensor_copy(v1[:, nxt, 0, :, 0:DH], vf[:]).then_inc(s["vh_ok"], 1)
                    ge(dve, s["vh_ok"], k + 2)
                    nc.vector.tensor_tensor(v1[:, nxt, 1, :, 0:DH], vf[:], v1[:, nxt, 0, :, 0:DH], ALU.subtract)\
                        .then_inc(s["v_ok"], 1)
                if back:
                    ge(dve, s["y_mm"], k)
                    nc.vector.tensor_tensor(yb[:], pY, bo[:], ALU.add).then_inc(s["yb_ok"], 1)
                    ge(dve, s["yb_ok"], k)
                    nc.vector.tensor_tensor(h2_all[:, k - 1, :], yb[:], h2_all[:, k - 1, :], ALU.add)\
                        .then_inc(s["h2_ok"], 1)
                    ge(dve, s["h2_ok"], k)
                    nc.vector.tensor_copy(touch[:], mv0[:, 0:1])
                    stats(k - 1, 2, h2_all[:, k - 1, :], st2, mv2, ve2)
                if front:
                    ge(dve, s["s_mm"], k + 1)
                    ge(dve, s["qkb_mm"], k + 2)
                    masked(Y, qkm[:, 1], "qkmb_ok")
                if back:
                    ge(dve, s["r2_ok"], k)
                    ge(dve, s["x2c_ok"], k - 1)
                    ge(dve, s["x2_tr"], k - 1)
                    nc.vector.tensor_scalar(x2[:], h2_all[:, k - 1, :], mv2[:, 0:1], r2[:], ALU.subtract, ALU.mult)\
                        .then_inc(s["x2_ok"], 1)
                if front:
                    ge(dve, s["qka_mm"], k + 2)
                    masked(X, qkm[:, 0], "qkma_ok")
                    ge(dve, s["cwT_mm"], k + 2)
                    nc.vector.tensor_reduce(mx[:], Z.rearrange("p (n s) -> p n s", s=S), AX.X, ALU.max)\
                        .then_inc(s["mx_ok"], 1)
                    ge(dve, s["mx_ok"], k + 2)
                    ge(dve, s["cwT_ok"], k + 1)
                    nc.vector.tensor_tensor(cwd[:, :, :].rearrange("p j (n s) -> p (j n) s", s=S),
                                            Z.rearrange("p (n s) -> p n s", s=S), bc(mx[:, :], [P, P, S]), ALU.subtract)\
                        .then_inc(s["cwd_ok"], 1)
                if mid:
                    ge(dve, s["amla_ok"], k)
                    ge(dve, s["amlb_ok"], k)
                    ge(dve, s["aa_mm"], k + 1)
                    masked(X, am[:, 0], "ama_ok")
                    ge(dve, s["ab_mm"], k + 1)
                    masked(Y, am[:, 1], "amb_ok")

            steps(dve, step)


def gated_unit_buffers(nc, ctx, tag, ps):

    def sb(name, shape, dt=F32):
        return ctx.enter_context(nc.sbuf_tensor(tag + name, shape, dt))

    u = {
        "xT": sb("xT", [P, 2, KD, P]), "sil": sb("sil", [P, 2, HE]), "h": sb("h", [P, 2, HE]),
        "hT": sb("hT", [P, KH, P]),
        "gate": [ps[:, 0:HE], ps[:, 512:512 + HE]], "up": [ps[:, 1024:1024 + HE], ps[:, 1536:1536 + HE]],
        "pHT": ps[:, 2048:2048 + KH * P], "y": [ps[:, 2560:2560 + D], ps[:, 3072:3072 + D]],
        "pXT": ps[:, 3584:3584 + KD * P],
    }
    for n in "gate_mm up_mm h_tr y_mm xT_ok sil_ok h_ok hT_ok y_ok".split():
        u[n] = ctx.enter_context(nc.semaphore(tag + n))
    return u


def tensor_gate(nc, pe, u, n, par, w):
    ge(pe, u["xT_ok"], n + 1)
    ge(pe, u["sil_ok"], n - 1)
    for c in range(KD):
        last = nc.tensor.matmul(u["gate"][par], u["xT"][:, par, c, :], w(c)[0], start=c == 0, stop=c == KD - 1)
    last.then_inc(u["gate_mm"], 1)


def tensor_up(nc, pe, u, n, par, w):
    ge(pe, u["h_ok"], n - 1)
    for c in range(KD):
        last = nc.tensor.matmul(u["up"][par], u["xT"][:, par, c, :], w(c)[1], start=c == 0, stop=c == KD - 1)
    last.then_inc(u["up_mm"], 1)


def tensor_transpose_h(nc, pe, u, n, par, ident):
    ge(pe, u["h_ok"], n + 1)
    ge(pe, u["hT_ok"], n)
    for c in range(KH):
        last = nc.tensor.transpose(u["pHT"][0:HK[c], c * P:(c + 1) * P], u["h"][:, par, c * P:c * P + HK[c]], ident[:])
    last.then_inc(u["h_tr"], 1)


def tensor_down(nc, pe, u, n, par, w3):
    ge(pe, u["hT_ok"], n + 1)
    ge(pe, u["y_ok"], n - 1)
    for c in range(KH):
        last = nc.tensor.matmul(u["y"][par], u["hT"][0:HK[c], c, :], w3(c), start=c == 0, stop=c == KH - 1)
    last.then_inc(u["y_mm"], 1)


def scalar_silu(nc, act, u, n, par):
    ge(act, u["gate_mm"], n + 1)
    ge(act, u["h_ok"], n - 1)
    nc.scalar.activation(u["sil"][:, par, :], u["gate"][par], ACT.Silu).then_inc(u["sil_ok"], 1)


def scalar_hT(nc, act, u, n):
    ge(act, u["h_tr"], n + 1)
    ge(act, u["y_mm"], n)
    nc.scalar.activation(u["hT"][:, 0:KH - 1, :], u["pHT"][:, 0:(KH - 1) * P], ACT.Copy)
    nc.scalar.activation(u["hT"][0:HK[-1], KH - 1, :], u["pHT"][0:HK[-1], (KH - 1) * P:KH * P], ACT.Copy)\
        .then_inc(u["hT_ok"], 1)


def vector_h(nc, dve, u, n, par):
    ge(dve, u["up_mm"], n + 1)
    ge(dve, u["sil_ok"], n + 1)
    ge(dve, u["h_tr"], n - 1)
    nc.vector.tensor_tensor(u["h"][:, par, :], u["sil"][:, par, :], u["up"][par], ALU.mult).then_inc(u["h_ok"], 1)


def pairs(eng, body, count):
    for k in range(-1, 2):
        body(k, k % 2)
    loops = (count - 3) // 2
    with eng.Fori(1, 1 + loops) as i:
        body(i * 2, 0)
        body(i * 2 + 1, 1)
    for k in range(2 + 2 * loops, count):
        body(k, k % 2)


def shared_stage(nc, ctx, io, keep):

    def sb(name, shape, dt=F32):
        return ctx.enter_context(nc.sbuf_tensor(name, shape, dt))

    def sem(name):
        return ctx.enter_context(nc.semaphore(name))

    ident, x2_all, x2T_all, lg_all, h2_all, ps = (keep[n] for n in ("ident", "x2", "x2T", "lg", "h2", "ps"))
    slots, prob, tile_expert = keep["slots"], keep["prob"], keep["tile_expert"]
    ws12, ws3 = keep["ws12"], keep["ws3"]

    u = gated_unit_buffers(nc, ctx, "sh_", ps)
    strict, ones = sb("strict", [P, P]), sb("ones", [P, P])
    rc = sb("rc", [P, RC])
    thr, rev, tile_no = rc[:, 0:NT], rc[:, NT:NT + E], rc[:, NT + E:RC]
    names = """lga rank oneh1 oneh2 lgb rankb oneh picked tot grid gsel""".split()
    b = {n: sb("r_" + n, [P, E, NT]) for n in names}
    m1, m2, f1, f2, dm = (sb("r_" + n, [P, NT]) for n in "m1 m2 f1 f2 dm".split())
    cum, ones_row = sb("cum", [P, E * NT]), sb("ones_row", [P, E * NT])
    cmp16, cnt, nt, ntI, base, off = (sb("r_" + n, [P, E, NT] if n == "cmp16" else [P, E])
                                      for n in "cmp16 cnt nt ntI base off".split())
    tcmp, tex = sb("tcmp", [P, NS, E]), sb("tex", [P, NS])
    slotf = sb("slotf", [P, NT, 2])

    r_in, r_ok, r_mm, r_e = sem("B_r_in"), sem("B_r_ok"), sem("B_r_mm"), sem("B_r_e")
    slot_ok, sent, rows_out = sem("B_slot_ok"), sem("B_sent"), sem("B_rows_out")
    pR, pTot = ps[:, 2560:2560 + P], ps[:, 3072:3072 + P]

    UN = 2 * NT

    with nc.Block() as block:

        @block.sync
        def _(sp):
            for dst, src in ((strict, io["strict"]), (ones, io["ones"]), (rc, io["rc"])):
                sp.dma_start(dst[:], src).then_inc(r_in, 16)
            sp.dma_start(keep["w12"][:], io["w12"]).then_inc(keep["w_in"], 16)
            sp.dma_start(keep["w3"][:], io["w3"]).then_inc(keep["w_in"], 16)
            sp.wait_ge(slot_ok, 1)
            for rows, part, image in ((keep["slot_rows"], slots, keep["image_slots"]),
                                      (keep["prob_rows"], prob, keep["image_prob"])):
                sp.dma_start(rows.rearrange("(t p) n -> p t n", p=P), part[:]).then_inc(rows_out, 16)
            sp.wait_ge(rows_out, 32)
            for rows, part, image in ((keep["slot_rows"], slots, keep["image_slots"]),
                                      (keep["prob_rows"], prob, keep["image_prob"])):
                sp.dma_start(image[:], rows.rearrange("(r p s) n -> p r s n", p=P, s=S)).then_inc(rows_out, 16)
            hb = keep["hb"].rearrange("s (t n) d -> t n s d", t=NT)
            with sp.Fori(0, NT) as t:
                sp.wait_ge(u["y_ok"], t * 2 + 2)
                sp.dma_start(hb[t], h2_all[:, t, :]).then_inc(keep["h_out"], 16)
            sp.wait_ge(rows_out, 64)

        @block.tensor
        def _(pe):
            pe.wait_ge(r_in, 48)
            pe.wait_ge(r_ok, ONEHOT)
            onehot = b["oneh"][:, :, :].rearrange("p e t -> p (e t)")
            nc.tensor.matmul(pR, strict[:], onehot, start=True, stop=True)
            nc.tensor.matmul(pTot, ones[:], onehot, start=True, stop=True).then_inc(r_mm, 1)
            pe.wait_ge(slot_ok, 1)

            def step(k, par):
                w = lambda c: (ws12[:, 1 - par, c, 0:HE], ws12[:, 1 - par, c, HE:2 * HE])
                if has(k, -1, UN - 1):
                    tensor_gate(nc, pe, u, k + 1, 1 - par, w)
                if has(k, 0, UN):
                    tensor_transpose_h(nc, pe, u, k, par, ident)
                if has(k, -1, UN - 1):
                    tensor_up(nc, pe, u, k + 1, 1 - par, w)
                if has(k, 0, UN):
                    tensor_down(nc, pe, u, k, par, lambda c: ws3[0:HK[c], par, c, :])

            pairs(pe, step, UN)

        @block.scalar
        def _(act):
            act.wait_ge(r_ok, DIFF)
            nc.scalar.activation(f2[:], dm[:], ACT.Exp).then_inc(r_e, 1)

            def step(k, par):
                if has(k, -1, UN - 1):
                    t = (k + 1) // 2 if isinstance(k, int) else None
                    ge(act, u["up_mm"], k)
                    src = x2T_all[:, t, :, :] if t is not None else x2T_all[:, tile_of[0] + par, :, :]
                    nc.scalar.activation(u["xT"][:, 1 - par], src, ACT.Copy).then_inc(u["xT_ok"], 1)
                    scalar_silu(nc, act, u, k + 1, 1 - par)
                if has(k, 0, UN):
                    scalar_hT(nc, act, u, k)

            tile_of = [None]
            for k in range(-1, 2):
                step(k, k % 2)
            loops = (UN - 3) // 2
            with act.Fori(1, 1 + loops) as i:
                tile_of[0] = i
                step(i * 2, 0)
                step(i * 2 + 1, 1)
            for k in range(2 + 2 * loops, UN):
                step(k, k % 2)

        @block.vector
        def _(dve):
            v = nc.vector
            done = [0]

            def link(ins):
                done[0] += 1
                ins.then_inc(r_ok, 1)
                dve.wait_ge(r_ok, done[0])

            def over_e(ap):
                return ap.rearrange("p e t -> p t e")

            def each_e(ap):
                return ap.unsqueeze(1).broadcast_to([P, E, NT])

            def first_of(logits, m, eq, rank, fi, onehot):
                link(v.tensor_reduce(m[:], over_e(logits), AX.X, ALU.max))
                link(v.tensor_tensor(eq[:], logits, each_e(m[:, :]), ALU.is_equal))
                link(v.tensor_tensor(rank[:], eq[:], bc(rev, [P, E, NT]), ALU.mult))
                link(v.tensor_reduce(fi[:], over_e(rank[:, :, :]), AX.X, ALU.max))
                link(v.tensor_tensor(onehot[:], bc(rev, [P, E, NT]), each_e(fi[:, :]), ALU.is_equal))

            dve.wait_ge(r_in, 48)
            link(v.tensor_copy(b["lga"][:], lg_all[:, :, :].rearrange("p t e -> p e t")))
            first_of(b["lga"][:, :, :], m1, b["gsel"], b["rank"], f1, b["oneh1"])
            link(v.scalar_tensor_tensor(b["lgb"][:, :, :].rearrange("p e t -> p (e t)"),
                                        b["oneh1"][:, :, :].rearrange("p e t -> p (e t)"), -1e30,
                                        b["lga"][:, :, :].rearrange("p e t -> p (e t)"), ALU.mult, ALU.add))
            first_of(b["lgb"][:, :, :], m2, b["picked"], b["rankb"], f1, b["oneh2"])
            link(v.tensor_tensor(b["oneh"][:], b["oneh1"][:], b["oneh2"][:], ALU.add))
            assert done[0] == ONEHOT
            link(v.tensor_tensor(dm[:], m2[:], m1[:], ALU.subtract))
            assert done[0] == DIFF
            link(v.memset(ones_row[:], 1.0))
            dve.wait_ge(r_mm, 1)
            link(v.tensor_copy(b["tot"][:, :, :].rearrange("p e t -> p (e t)"), pTot))
            link(v.tensor_tensor_scan(cum[:], ones_row[:], b["tot"][:, :, :].rearrange("p e t -> p (e t)"), 0.0,
                                      ALU.mult, ALU.add))
            link(v.tensor_reduce(cnt[:], b["tot"][:], AX.X, ALU.add))
            link(v.tensor_tensor(cmp16[:], bc(cnt[:, :], [P, E, NT]), each_e(thr), ALU.is_gt))
            link(v.tensor_reduce(nt[:], cmp16[:], AX.X, ALU.add))
            link(v.tensor_tensor_scan(ntI[:], ones_row[:, 0:E], nt[:], 0.0, ALU.mult, ALU.add))
            link(v.tensor_tensor(base[:], ntI[:], nt[:], ALU.subtract))
            link(v.tensor_tensor(off[:], cum[:, :].rearrange("p (e t) -> p e t", t=NT)[:, :, NT - 1], cnt[:], ALU.subtract))
            link(v.scalar_tensor_tensor(off[:], base[:], float(P), off[:], ALU.mult, ALU.subtract))
            link(v.tensor_tensor(b["grid"][:, :, :].rearrange("p e t -> p (e t)"), pR, cum[:], ALU.add))
            link(v.tensor_tensor(b["grid"][:], b["grid"][:], b["tot"][:], ALU.subtract))
            link(v.tensor_tensor(b["grid"][:], b["grid"][:], bc(off[:, :], [P, E, NT]), ALU.add))
            for n in range(2):
                link(v.tensor_tensor(b["gsel"][:], b["grid"][:], b[f"oneh{n + 1}"][:], ALU.mult))
                link(v.tensor_reduce(slotf[:, :, n], over_e(b["gsel"][:, :, :]), AX.X, ALU.add))
            link(v.tensor_copy(slots[:], slotf[:]))
            link(v.tensor_tensor(tcmp[:], bc(tile_no, [P, NS, E]), ntI[:, :].unsqueeze(1).broadcast_to([P, NS, E]),
                                 ALU.is_ge))
            link(v.tensor_reduce(tex[:], tcmp[:], AX.X, ALU.add))
            link(v.tensor_scalar(tile_expert[:], tex[:], float(E - 1), None, ALU.min))
            dve.wait_ge(r_e, 1)
            link(v.tensor_scalar(m1[:], f2[:], 1.0, None, ALU.add))
            link(v.reciprocal(prob[:, :, 0], m1[:]))
            link(v.tensor_tensor(prob[:, :, 1], prob[:, :, 0], f2[:], ALU.mult))
            v.memset(dm[:], 0.0).then_inc(slot_ok, 1)

            def step(k, par):
                if has(k, -1, UN - 1):
                    vector_h(nc, dve, u, k + 1, 1 - par)
                if has(k, 0, UN):
                    t = k // 2 if isinstance(k, int) else tile_of[0]
                    ge(dve, u["y_mm"], k + 1)
                    ge(dve, u["y_ok"], k)
                    v.tensor_tensor(h2_all[:, t, :], h2_all[:, t, :], u["y"][par], ALU.add).then_inc(u["y_ok"], 1)

            tile_of = [None]
            for k in range(-1, 2):
                step(k, k % 2)
            loops = (UN - 3) // 2
            with dve.Fori(1, 1 + loops) as i:
                tile_of[0] = i
                step(i * 2, 0)
                step(i * 2 + 1, 1)
            for k in range(2 + 2 * loops, UN):
                step(k, k % 2)

        @block.gpsimd
        def _(pool):
            pool.wait_ge(slot_ok, 1)
            pool.wait_ge(keep["xs_zero"], 16)
            for t in range(NT):
                for n in range(2):
                    nc.gpsimd.indirect_dma_start(
                        out=keep["xs"], out_offset=bass.IndirectOffsetOnAxis(ap=slots[:, t, n:n + 1], axis=0),
                        in_=x2_all[:, t, :], in_offset=None).then_inc(sent, 16)
            pool.wait_ge(sent, 16 * 2 * NT)


def routed_stage(nc, ctx, io, keep):

    def sb(name, shape, dt=F32):
        return ctx.enter_context(nc.sbuf_tensor(name, shape, dt))

    def sem(name):
        return ctx.enter_context(nc.semaphore(name))

    ident, ps, tile_expert = keep["ident"], keep["ps"], keep["tile_expert"]
    w12, w3 = keep["w12"], keep["w3"]
    u = gated_unit_buffers(nc, ctx, "ro_", ps)
    xr = sb("xr", [P, 2, D])
    yo = sb("yo", [P, 2, D])
    xr_in = [sem("C_xr_in0"), sem("C_xr_in1")]
    y_out = [sem("C_y_out0"), sem("C_y_out1")]
    x_tr = sem("C_x_tr")
    xs = keep["xs"].rearrange("(j p) d -> j p d", p=P)
    ys = keep["ys"].rearrange("(j p) d -> j p d", p=P)

    with nc.Block() as block:

        def run(eng, body):
            for k in range(-2, 2):
                body(k, k % 2, k // 2)
            loops = (NS - 4) // 2
            with eng.Fori(1, 1 + loops) as i:
                body(i * 2, 0, i)
                body(i * 2 + 1, 1, i)
            for k in range(2 + 2 * loops, NS):
                body(k, k % 2, k // 2)

        @block.sync
        def _(sp):
            def step(k, par, i):
                if has(k, -2, NS - 2):
                    ge(sp, x_tr, k + 1)
                    sp.dma_start(xr[:, par, :], xs[k + 2]).then_inc(xr_in[par], 16)

            run(sp, step)
            sp.wait_ge(keep["h_out"], 16 * NT)

        @block.gpsimd
        def _(pool):
            def step(k, par, i):
                if has(k, 0, NS):
                    ge(pool, u["y_ok"], k + 1)
                    pool.dma_start(ys[k], yo[:, par, :]).then_inc(y_out[par], 16)

            run(pool, step)
            pool.wait_ge(y_out[0], 16 * ((NS + 1) // 2))
            pool.wait_ge(y_out[1], 16 * (NS // 2))

        @block.tensor
        def _(pe):
            pe.wait_ge(keep["w_in"], 32)

            def expert(k):
                return pe.value_load(tile_expert[0:1, k:k + 1] if isinstance(k, int) else
                                     tile_expert[0:1, bass.ds(k, 1)], min_val=0, max_val=E - 1)

            e_of = {}

            def step(k, par, i):
                if has(k, -1, NS - 1):
                    e = expert(k + 1)
                    e_of[1 - par] = e
                    w = lambda c: (w12[:, e, c, 0:HE], w12[:, e, c, HE:2 * HE])
                    tensor_gate(nc, pe, u, k + 1, 1 - par, w)
                if has(k, 0, NS):
                    tensor_transpose_h(nc, pe, u, k, par, ident)
                if has(k, -1, NS - 1):
                    tensor_up(nc, pe, u, k + 1, 1 - par, w)
                if has(k, -2, NS - 2):
                    ge(pe, xr_in[par], 16 * (i + 2))
                    ge(pe, u["xT_ok"], k + 2)
                    for c in range(KD):
                        last = nc.tensor.transpose(u["pXT"][:, c * P:(c + 1) * P], xr[:, par, c * P:(c + 1) * P], ident[:])
                    last.then_inc(x_tr, 1)
                if has(k, 0, NS):
                    e2 = expert(k)
                    tensor_down(nc, pe, u, k, par, lambda c: w3[0:HK[c], e2, c, :])

            run(pe, step)

        @block.scalar
        def _(act):
            def step(k, par, i):
                if has(k, -1, NS - 1):
                    scalar_silu(nc, act, u, k + 1, 1 - par)
                if has(k, 0, NS):
                    scalar_hT(nc, act, u, k)
                if has(k, -2, NS - 2):
                    ge(act, x_tr, k + 3)
                    ge(act, u["up_mm"], k + 1)
                    nc.scalar.activation(u["xT"][:, par], u["pXT"], ACT.Copy).then_inc(u["xT_ok"], 1)

            run(act, step)

        @block.vector
        def _(dve):
            def step(k, par, i):
                if has(k, -1, NS - 1):
                    vector_h(nc, dve, u, k + 1, 1 - par)
                if has(k, 0, NS):
                    ge(dve, u["y_mm"], k + 1)
                    ge(dve, y_out[par], 16 * i)
                    nc.vector.tensor_copy(yo[:, par, :], u["y"][par]).then_inc(u["y_ok"], 1)

            run(dve, step)


def final_stage(nc, ctx, io, keep):

    def sb(name, shape, dt=F32):
        return ctx.enter_context(nc.sbuf_tensor(name, shape, dt))

    def sem(name):
        return ctx.enter_context(nc.semaphore(name))

    ident, ps, slots, prob = (keep[n] for n in ("ident", "ps", "image_slots", "image_prob"))
    R = N // P
    wT, a1, a2, wc = (sb("L_" + n, [P, KD, D]) for n in ("wT", "a1", "a2", "wc"))
    ut = sb("ut", [P, KD, D])
    bias = sb("bias", [1, D])
    ones, mhalf, touch = sb("L_ones", [P, P]), sb("L_mhalf", [P, R]), sb("L_touch", [P, 1])
    w_in, w_ok, w_mm, c_ok = (sem("D_" + n) for n in "w_in w_ok w_mm c_ok".split())
    hin, gat = sb("hin", [P, 2, R, D]), sb("gat", [P, 2, R, 2, D])
    h3a, h3 = sb("h3a", [P, R, D]), sb("h3", [P, 3, R, D])
    st3, mv3, ve3, r3 = sb("st3", [P, R, 6]), sb("mv3", [P, R, 2]), sb("ve3", [P, R]), sb("r3", [P, R])
    st4, mv4, ve4, r4 = sb("st4", [P, R, 6]), sb("mv4", [P, R, 2]), sb("ve4", [P, R]), sb("r4", [P, R])
    x3 = sb("x3", [P, 3, R, D])
    vr, vr2, ss, rin = sb("vr", [P, R]), sb("vr2", [P, R]), sb("ss", [P, R]), sb("rin", [P, 2, R])
    diag = sb("diag", [P, R, P])
    x3T = sb("x3T", [P, KD, N])
    fac = sb("fac", [P, R, N])
    sim = sb("sim", [P, R, N])
    nm = sb("nm", [P, R])
    pr = sb("pr", [P, R, N])
    sm, rs = sb("sm", [P, R]), sb("rs", [P, 2, R])
    pT = sb("pT", [P, R, N])
    av = sb("av", [P, R, D])
    h4 = sb("h4", [P, 2, R, D])
    x4 = sb("x4", [P, R, D])
    x4T = sb("x4T", [P, KD, N])
    th = sb("th", [P, R, D])
    ho = sb("ho", [P, 2, R, D])
    pT3, pRow, pDot, pPT, pAV, pT4, pY, pW = (ps[:, 512 * n:512 * (n + 1)] for n in range(8))
    names = """x3_tr row_mm dot_mm p_tr av_mm x4_tr y_mm  x3T_ok p_ok pT_ok x4T_ok th_ok h3a_ok h3_ok
        st3_ok mv3_ok ve3_ok r3_ok x3_ok vr_ok vr2_ok ss_ok rin_ok diag_ok fac_ok sim_ok nm_ok rs_ok av_ok h4_ok
        st4_ok mv4_ok ve4_ok r4_ok x4_ok ho_ok""".split()
    s = {n: sem("E_" + n) for n in names}
    h_in, gath, o_out = ([sem(f"E_{n}{par}") for par in range(2)] for n in ("h_in", "gath", "o_out"))

    with nc.Block() as block:

        def run(body):
            for k in range(-2, S + 3):
                body(k, k % 2, k // 2)

        hb = keep["hb"].rearrange("s (r p) d -> s p r d", p=P)
        ob = io["out"].rearrange("s (r p) d -> s p r d", p=P)

        @block.sync
        def _(sp):
            for n in range(2):
                sp.dma_start(hin[:, n], hb[n]).then_inc(h_in[n], 16)
            for dst, src in ((wT, io["l1w"]), (a1, io["l1a1"]), (a2, io["l1a2"]),
                             (bias, io["l1b"].unsqueeze(0)), (ones, io["ones"])):
                sp.dma_start(dst[:], src).then_inc(w_in, 16)

            def step(k, par, i):
                if has(k, -2, S - 4):
                    ge(sp, s["h3a_ok"], k + 3)
                    sp.dma_start(hin[:, par], hb[k + 4]).then_inc(h_in[par], 16)
                if has(k - 3, 0, S):
                    ge(sp, s["ho_ok"], k - 2)
                    sp.dma_start(ob[k - 3], ho[:, 1 - par]).then_inc(o_out[1 - par], 16)

            run(step)
            for par in range(2):
                sp.wait_ge(o_out[par], 16 * (S // 2))

        @block.tensor
        def _(pe):
            mm, tr = nc.tensor.matmul, nc.tensor.transpose
            pe.wait_ge(w_in, 80)
            for out, left, right, n in ((pY, a1, wT, 0), (pW, ut, a2, 1)):
                ge(pe, w_ok, n)
                for m in range(KD):
                    for c in range(KD):
                        last = mm(out[:, m * D:(m + 1) * D], left[:, c, m * P:(m + 1) * P], right[:, c, :],
                                  start=c == 0, stop=c == KD - 1)
                last.then_inc(w_mm, 1)

            def transposes(out, src):
                for c in range(KD):
                    for r in range(R):
                        last = tr(out[:, c * N + r * P:c * N + (r + 1) * P], src[:, r, c * P:(c + 1) * P], ident[:])
                return last

            def step(k, par, i):
                nxt = 1 - par
                if has(k - 1, 0, S):
                    ge(pe, s["p_ok"], k)
                    ge(pe, s["pT_ok"], k - 1)
                    transposes(pPT, pr).then_inc(s["p_tr"], 1)
                if has(k - 2, 0, S):
                    ge(pe, s["x4_ok"], k - 1)
                    ge(pe, s["x4T_ok"], k - 2)
                    transposes(pT4, x4).then_inc(s["x4_tr"], 1)
                if has(k - 1, 0, S):
                    ge(pe, s["pT_ok"], k)
                    ge(pe, s["av_ok"], k - 1)
                    for r in range(R):
                        for c in range(R):
                            last = mm(pAV[:, r * D:(r + 1) * D], pT[:, c, r * P:(r + 1) * P], x3[:, (k - 1) % 3, c, :],
                                      start=c == 0, stop=c == R - 1)
                    last.then_inc(s["av_mm"], 1)
                if has(k, -1, S - 1):
                    ge(pe, s["x3_ok"], k + 2)
                    ge(pe, s["x3T_ok"], k + 1)
                    transposes(pT3, x3[:, (k + 1) % 3]).then_inc(s["x3_tr"], 1)
                    ge(pe, s["diag_ok"], k + 2)
                    ge(pe, s["fac_ok"], k + 1)
                    mm(pRow[:, 0:N], ones[:], diag[:, :, :].rearrange("p r n -> p (r n)"), start=True, stop=True)\
                        .then_inc(s["row_mm"], 1)
                    ge(pe, s["x3T_ok"], k + 2)
                    ge(pe, s["sim_ok"], k + 1)
                    for r in range(R):
                        for c in range(KD):
                            last = mm(pDot[:, r * N:(r + 1) * N], x3T[:, c, r * P:(r + 1) * P], x3T[:, c, :],
                                      start=c == 0, stop=c == KD - 1)
                    last.then_inc(s["dot_mm"], 1)
                if has(k - 2, 0, S):
                    ge(pe, w_ok, 2)
                    ge(pe, s["x4T_ok"], k - 1)
                    ge(pe, s["th_ok"], k - 2)
                    for r in range(R):
                        for c in range(KD):
                            mm(pY[:, r * D:(r + 1) * D], x4T[:, c, r * P:(r + 1) * P], wc[:, c, :],
                               start=c == 0, stop=False)
                        last = mm(pY[:, r * D:(r + 1) * D], ones[0:1, :], bias[0:1, :], start=False, stop=True)
                    last.then_inc(s["y_mm"], 1)

            run(step)

        @block.scalar
        def _(act):
            for n, (dst, src) in enumerate(((ut, pY), (wc, pW))):
                act.wait_ge(w_mm, n + 1)
                nc.scalar.activation(dst[:], src, ACT.Copy).then_inc(w_ok, 1)

            def step(k, par, i):
                if has(k - 1, 0, S):
                    ge(act, s["p_tr"], k)
                    ge(act, s["av_mm"], k - 1)
                    nc.scalar.activation(pT[:], pPT, ACT.Copy).then_inc(s["pT_ok"], 1)
                if has(k, 0, S):
                    ge(act, s["nm_ok"], k + 1)
                    ge(act, s["p_tr"], k)
                    ge(act, s["rs_ok"], k)
                    for r in range(R):
                        last = nc.scalar.activation(pr[:, r, :], sim[:, r, :], ACT.Exp, bias=nm[:, r:r + 1],
                                                    accum_out=sm[:, r:r + 1])
                    last.then_inc(s["p_ok"], 1)
                if has(k, -1, S - 1):
                    ge(act, s["x3_tr"], k + 2)
                    ge(act, s["dot_mm"], k + 1)
                    nc.scalar.activation(x3T[:], pT3, ACT.Copy).then_inc(s["x3T_ok"], 1)
                if has(k - 2, 0, S):
                    ge(act, s["x4_tr"], k - 1)
                    ge(act, s["y_mm"], k - 2)
                    nc.scalar.activation(x4T[:], pT4, ACT.Copy).then_inc(s["x4T_ok"], 1)
                    ge(act, s["y_mm"], k - 1)
                    ge(act, s["ho_ok"], k - 2)
                    nc.scalar.activation(th[:], pY.rearrange("p (r d) -> p r d", r=R), ACT.Tanh).then_inc(s["th_ok"], 1)

            run(step)

        @block.gpsimd
        def _(pool):
            pl = nc.gpsimd

            def gather(t):
                ge(pool, s["h3_ok"], t - 1)
                for r in range(R):
                    for n in range(2):
                        pl.indirect_dma_start(
                            out=gat[:, t % 2, r, n, :], out_offset=None, in_=keep["ys"],
                            in_offset=bass.IndirectOffsetOnAxis(ap=slots[:, r, t, n:n + 1], axis=0))\
                            .then_inc(gath[t % 2], 16)

            def power(t, n, src, dst):
                ge(pool, s[n], t + 1)
                return pl.tensor_tensor(dst, src, mhalf[:], ALU.pow)

            def step(k, par, i):
                if has(k, -1, S - 1):
                    power(k + 1, "ve3_ok", ve3[:], r3[:]).then_inc(s["r3_ok"], 1)
                    power(k + 1, "ss_ok", ss[:], rin[:, 1 - par, :]).then_inc(s["rin_ok"], 1)
                if has(k - 3, 0, S):
                    ge(pool, s["th_ok"], k - 2)
                    ge(pool, o_out[1 - par], 16 * (i + par - 2))
                    pl.tensor_tensor(ho[:, 1 - par], th[:], h4[:, 1 - par], ALU.add).then_inc(s["ho_ok"], 1)
                if has(k - 1, 0, S):
                    power(k - 1, "ve4_ok", ve4[:], r4[:]).then_inc(s["r4_ok"], 1)
                if has(k, -2, S - 3):
                    gather(k + 3)

            pl.memset(mhalf[:], -0.5).then_inc(c_ok, 1)
            pool.wait_ge(c_ok, 1)
            gather(0)
            run(step)

        @block.vector
        def _(dve):
            v = nc.vector

            def stats(t, n, src, st, mv, ve):
                for r in range(R):
                    last = v.bn_stats(st[:, r, :], src[:, r, :])
                last.then_inc(s[f"st{n}_ok"], 1)
                ge(dve, s[f"st{n}_ok"], t + 1)
                v.tensor_copy(touch[:], st[:, 0, 0:1])
                for r in range(R):
                    last = v.bn_aggr(mv[:, r, :], st[:, r, :])
                last.then_inc(s[f"mv{n}_ok"], 1)
                ge(dve, s[f"mv{n}_ok"], t + 1)
                ge(dve, s[f"r{n}_ok"], t)
                v.tensor_scalar(ve[:], mv[:, :, 1], EPS, None, ALU.add).then_inc(s[f"ve{n}_ok"], 1)

            def normed(t, n, dst, src, mv, rr):
                ge(dve, s[f"r{n}_ok"], t + 1)
                for r in range(R):
                    last = v.tensor_scalar(dst[:, r, :], src[:, r, :], mv[:, r, 0:1], rr[:, r:r + 1],
                                           ALU.subtract, ALU.mult)
                last.then_inc(s[f"x{n}_ok"], 1)

            def step(k, par, i):
                nxt = 1 - par
                if has(k, -1, S - 1):
                    ge(dve, s["h3_ok"], k + 2)
                    stats(k + 1, 3, h3[:, (k + 1) % 3], st3, mv3, ve3)
                    ge(dve, s["r3_ok"], k + 2)
                    v.tensor_tensor(vr[:], mv3[:, :, 1], r3[:], ALU.mult).then_inc(s["vr_ok"], 1)
                    ge(dve, s["vr_ok"], k + 2)
                    ge(dve, s["rin_ok"], k + 1)
                    v.tensor_tensor(vr2[:], vr[:], r3[:], ALU.mult).then_inc(s["vr2_ok"], 1)
                    ge(dve, s["vr2_ok"], k + 2)
                    v.tensor_scalar(ss[:], vr2[:], float(D), 1e-36, ALU.mult, ALU.max).then_inc(s["ss_ok"], 1)
                if has(k, 0, S):
                    ge(dve, s["row_mm"], k + 1)
                    for r in range(R):
                        last = v.tensor_scalar(fac[:, r, :], pRow[:, 0:N], rin[:, par, r:r + 1], 1e8, ALU.mult, ALU.min)
                    last.then_inc(s["fac_ok"], 1)
                    ge(dve, s["dot_mm"], k + 1)
                    ge(dve, s["fac_ok"], k + 1)
                    ge(dve, s["p_ok"], k)
                    v.tensor_tensor(sim[:], pDot.rearrange("p (r n) -> p r n", r=R), fac[:], ALU.mult)\
                        .then_inc(s["sim_ok"], 1)
                    ge(dve, s["sim_ok"], k + 1)
                    v.tensor_reduce(nm[:], sim[:], AX.X, ALU.max, negate=True).then_inc(s["nm_ok"], 1)
                if has(k, -1, S - 1):
                    ge(dve, s["av_mm"], k - 1)
                    normed(k + 1, 3, x3[:, (k + 1) % 3], h3[:, (k + 1) % 3], mv3, r3)
                    ge(dve, s["rin_ok"], k + 2)
                    ge(dve, s["row_mm"], k + 1)
                    for r in range(R):
                        last = v.tensor_scalar(diag[:, r, :], ident[:], rin[:, nxt, r:r + 1], None, ALU.mult)
                    last.then_inc(s["diag_ok"], 1)
                if has(k - 1, 0, S):
                    ge(dve, s["av_mm"], k)
                    ge(dve, s["rs_ok"], k)
                    for r in range(R):
                        last = v.scalar_tensor_tensor(av[:, r, :], pAV[:, r * D:(r + 1) * D], rs[:, nxt, r:r + 1],
                                                      x3[:, (k - 1) % 3, r, :], ALU.mult, ALU.add)
                    last.then_inc(s["av_ok"], 1)
                    ge(dve, s["av_ok"], k)
                    ge(dve, s["ho_ok"], k - 2)
                    v.tensor_tensor(h4[:, nxt], av[:], h3[:, (k - 1) % 3], ALU.add).then_inc(s["h4_ok"], 1)
                    ge(dve, s["h4_ok"], k)
                    stats(k - 1, 4, h4[:, nxt], st4, mv4, ve4)
                if has(k - 1, 0, S):
                    ge(dve, s["x4_tr"], k - 1)
                    normed(k - 1, 4, x4, h4[:, nxt], mv4, r4)
                if has(k, -2, S - 2):
                    t = k + 2
                    ge(dve, h_in[par], 16 * (i + 2))
                    ge(dve, gath[par], 32 * R * (i + 2))
                    ge(dve, s["h3_ok"], t)
                    for r in range(R):
                        last = v.scalar_tensor_tensor(h3a[:, r, :], gat[:, par, r, 0, :], prob[:, r, t, 0:1],
                                                      hin[:, par, r, :], ALU.mult, ALU.add)
                    last.then_inc(s["h3a_ok"], 1)
                    ge(dve, s["h3a_ok"], t + 1)
                    ge(dve, s["h4_ok"], k)
                    for r in range(R):
                        last = v.scalar_tensor_tensor(h3[:, t % 3, r, :], gat[:, par, r, 1, :], prob[:, r, t, 1:2],
                                                      h3a[:, r, :], ALU.mult, ALU.add)
                    last.then_inc(s["h3_ok"], 1)
                if has(k, 0, S):
                    ge(dve, s["p_ok"], k + 1)
                    v.reciprocal(rs[:, par, :], sm[:]).then_inc(s["rs_ok"], 1)

            run(step)


def build(nc, io):
    ctx = ExitStack()
    with ctx:
        def sb(name, shape, dt=F32):
            return ctx.enter_context(nc.sbuf_tensor(name, shape, dt))

        keep = {
            "ident": sb("ident", [P, P]), "mask": sb("mask", [P, P]),
            "h2": sb("h2_all", [P, NT, D]), "lg": sb("lg_all", [P, NT, E]),
            "slots": sb("slots", [P, NT, 2], I32), "prob": sb("prob", [P, NT, 2]),
            "image_slots": sb("image_slots", [P, N // P, S, 2], I32), "image_prob": sb("image_prob", [P, N // P, S, 2]),
            "tile_expert": sb("tile_expert", [P, NS], I32),
            "ps": ctx.enter_context(nc.psum_tensor("ps", [P, 4096], F32)),
            "xs": nc.dram_tensor("xs", (NS * P, D), F32, kind="Internal").ap(),
            "ys": nc.dram_tensor("ys", (NS * P, D), F32, kind="Internal").ap(),
            "slot_rows": nc.dram_tensor("slot_rows", (S * N, 2), I32, kind="Internal").ap(),
            "prob_rows": nc.dram_tensor("prob_rows", (S * N, 2), F32, kind="Internal").ap(),
            "hb": nc.dram_tensor("hb", (S, N, D), F32, kind="Internal").ap(),
        }
        for n in ("xs_zero", "ws_in", "w_in", "h_out"):
            keep[n] = ctx.enter_context(nc.semaphore(n))
        with ExitStack() as first:
            for n, shape in (("x2", [P, NT, D]), ("x2T", [P, NT, KD, P]), ("ws12", [P, 2, KD, 2 * HE]),
                             ("ws3", [P, 2, KH, D]), ("zeros", [P, D])):
                keep[n] = first.enter_context(nc.sbuf_tensor(n + "_all", shape, F32))
            with ExitStack() as stage:
                attention_stage(nc, stage, io, keep)
            for n, shape in (("w12", [P, E, KD, 2 * HE]), ("w3", [P, E, KH, D])):
                keep[n] = first.enter_context(nc.sbuf_tensor(n + "_all", shape, F32))
            with ExitStack() as stage:
                shared_stage(nc, stage, io, keep)
            with ExitStack() as stage:
                routed_stage(nc, stage, io, keep)
        with ExitStack() as stage:
            final_stage(nc, stage, io, keep)


def layout(inputs):
    a = {k: np.asarray(v) for k, v in inputs.items()}
    x = a["x"].reshape(S, 5, 16, 8, 16, 8)
    x = x.transpose(1, 3, 5, 2, 4, 0).reshape(FEAT, T)
    xp = np.zeros((KF * P, T), x.dtype)
    xp[:FEAT] = x
    xp = xp.reshape(KF, P, NT, P).transpose(2, 1, 0, 3)
    wt = np.zeros((KF * P, D), x.dtype)
    wt[:FEAT] = a["L0_tok_W"]

    def rows(m):
        return m.reshape(-1, P, m.shape[1]).transpose(1, 0, 2)

    qc = np.zeros((HP, P, P), x.dtype)
    q_c = a["L0_attn_q_c"].reshape(C, H, DH)
    for h in range(H):
        j, e = h // 2, h % 2
        qc[j, 32 * (j % 4) + DH * e:32 * (j % 4) + DH * (e + 1), C * e:C * (e + 1)] = q_c[:, h, :].T
    small = np.zeros((P, 8), x.dtype)
    small[:, 0:2] = a["L0_attn_bq"].reshape(KD, P).T
    small[:, 2:4] = a["L0_attn_bk"].reshape(KD, P).T
    small[:, 4:6] = np.repeat(a["L0_attn_beta"], DH).reshape(KD, P).T
    head = np.arange(P) // DH
    small[:, 6] = head % 2 == 0
    small[:, 7] = head % 2 == 1
    n, s = np.arange(P) // S, np.arange(P) % S
    mask = ((n[:, None] == n[None, :]) & (s[:, None] <= s[None, :])).astype(x.dtype)
    def chunks(m, k):
        full = np.zeros(m.shape[:-2] + (k * P, m.shape[-1]), m.dtype)
        full[..., :m.shape[-2], :] = m
        full = full.reshape(m.shape[:-2] + (k, P, m.shape[-1]))
        return np.moveaxis(full, -2, 0)

    w12 = np.concatenate([a["L0_ffn_W1"], a["L0_ffn_W2"]], -1)
    ws12 = np.stack([np.concatenate([a["L0_ffn_Ws1"][:, n * HE:(n + 1) * HE], a["L0_ffn_Ws2"][:, n * HE:(n + 1) * HE]], -1)
                     for n in range(2)])
    ws3 = a["L0_ffn_Ws3"].reshape(2, HE, D)
    rc = np.zeros((P, RC), x.dtype)
    rc[:, 0:NT] = np.arange(NT) * P
    rc[:, NT:NT + E] = E - np.arange(E)
    rc[:, NT + E:] = np.arange(NS)
    idx = np.arange(P)
    out = {
        "w12": chunks(w12, KD), "w3": chunks(a["L0_ffn_W3"], KH), "ws12": chunks(ws12, KD), "ws3": chunks(ws3, KH),
        "rc": rc, "strict": (idx[:, None] < idx[None, :]).astype(x.dtype), "ones": np.ones((P, P), x.dtype),
        "l1w": rows(a["L1_ffn_weight"].T), "l1a1": rows(a["L1_ffn_aux_weight1"]), "l1a2": rows(a["L1_ffn_aux_weight2"]),
        "l1b": a["L1_ffn_bias"],
        "x": xp, "wtok": rows(wt), "gamma": a["L0_tok_gamma"], "small": small, "qc": qc.transpose(1, 0, 2),
        "wq": rows(a["L0_attn_Wq"].T), "wk": rows(a["L0_attn_Wk"].T), "wv": rows(a["L0_attn_Wv"].T),
        "wo": rows(a["L0_attn_Wo"].T), "bv": a["L0_attn_bv"], "bo": a["L0_attn_bo"], "wg": rows(a["L0_ffn_Wg"]),
        "ident": np.eye(P, dtype=x.dtype), "mask": mask,
    }
    return {k: np.ascontiguousarray(v) for k, v in out.items()}


OUTS = {"out": (S, N, D)}


def kernel(**inputs):
    import concourse.bacc as bacc
    from concourse.bass_utils import run_bass_kernel_spmd

    arrays = layout(inputs)
    nc = bacc.Bacc("TRN2", target_bir_lowering=False, num_devices=1)
    io = {n: nc.dram_tensor("in_" + n, a.shape, mybir.dt.from_np(a.dtype), kind="ExternalInput").ap()
          for n, a in arrays.items()}
    for n, shape in OUTS.items():
        io[n] = nc.dram_tensor(n, shape, F32, kind="ExternalOutput").ap()
    build(nc, io)
    r = run_bass_kernel_spmd(nc, [{"in_" + n: a for n, a in arrays.items()}], core_ids=[0])
    return r.results[0]["out"]
```
